# Optimizing a Trainium2 kernel written in Bass

```python
import numpy as np
import jax
import jax.numpy as jnp

def _softmax(x, axis=-1):
    return jax.nn.softmax(x, axis=axis)

def _gelu(x):
    return jax.nn.gelu(x, approximate=True)

def _silu(x):
    return jax.nn.silu(x)

def _sigmoid(x):
    return jax.nn.sigmoid(x)

def _layernorm(x, axis=-1, eps=1e-05):
    m = jnp.mean(x, axis=axis, keepdims=True)
    v = jnp.var(x, axis=axis, keepdims=True)
    return (x - m) / jnp.sqrt(v + eps)

def _scatter_add(tgt, idx, src, axis=0):
    return tgt.at[idx].add(src)

def _segment_sum(src, seg, n):
    return jax.ops.segment_sum(src, seg, n)
kernel_name = 'mk_adj_resnorm_d2_adj_r2_1e5351'

def setup_inputs(seed: int=0):
    np.random.seed(seed)
    _w = jnp.asarray

    def _rec_inputs():
        import jax
        import jax.numpy as jnp
        _gk = jax.random.key(seed)
        x = -0.003407 + 1.001 * jax.random.normal(jax.random.fold_in(_gk, 1), (512, 128), jnp.float32)
        _a = jax.random.bernoulli(jax.random.fold_in(_gk, 2), 0.03125, (512, 512))
        _a = jnp.logical_or(_a, jnp.swapaxes(_a, -1, -2))
        _a = jnp.logical_or(_a, jnp.eye(512, dtype=bool))
        adj = _a.astype(jnp.int32)
        return (x, adj)
    x, adj = _rec_inputs()

    def _L0_gnn_setup():
        import jax, jax.numpy as jnp
        import numpy as np
        N = 512
        H = 128
        key = jax.random.key(seed)
        k1, k2, k3, k4, k5, k6, k7 = jax.random.split(key, 7)
        s = 1.0 / np.sqrt(H)
        node_features = jax.random.normal(k1, (N, H), dtype=jnp.float32)
        adjacency_matrix = jax.random.randint(k2, (N, N), 0, 2, dtype=jnp.int32)
        edge_table = jax.random.normal(k3, (N * N, H), dtype=jnp.float32)
        w_ih = jax.random.uniform(k4, (3 * H, H), minval=-s, maxval=s, dtype=jnp.float32)
        w_hh = jax.random.uniform(k5, (3 * H, H), minval=-s, maxval=s, dtype=jnp.float32)
        b_ih = jax.random.uniform(k6, (3 * H,), minval=-s, maxval=s, dtype=jnp.float32)
        b_hh = jax.random.uniform(k7, (3 * H,), minval=-s, maxval=s, dtype=jnp.float32)
        return {'node_features': node_features, 'adjacency_matrix': adjacency_matrix, 'edge_table': edge_table, 'w_ih': w_ih, 'w_hh': w_hh, 'b_ih': b_ih, 'b_hh': b_hh}
    _L0_gnn_all = _L0_gnn_setup()
    _L0_gnn_in = {k: v for k, v in _L0_gnn_all.items() if k in ('edge_table', 'w_ih', 'w_hh', 'b_ih', 'b_hh')}
    del _L0_gnn_all

    def _L1_gnn_setup():
        import jax, jax.numpy as jnp
        import numpy as np
        N = 6144
        IN_DIM = 128
        OUT_DIM = 128
        LR_SLOPE = 0.01
        NEG_INF = -9e+16
        key = jax.random.key(seed)
        k1, k2, k3, k4 = jax.random.split(key, 4)
        emb_mat = jax.random.normal(k1, (N, IN_DIM), dtype=jnp.float32)
        adj_mat = jax.random.randint(k2, (N, N), 0, 2, dtype=jnp.int32)
        W = jax.random.normal(k3, (OUT_DIM, IN_DIM), dtype=jnp.float32) * (2.0 / (IN_DIM + OUT_DIM)) ** 0.5
        a = jax.random.normal(k4, (2 * OUT_DIM, 1), dtype=jnp.float32) * (2.0 / (2 * OUT_DIM + 1)) ** 0.5
        return {'emb_mat': emb_mat, 'adj_mat': adj_mat, 'W': W, 'a': a}
    _L1_gnn_all = _L1_gnn_setup()
    _L1_gnn_in = {k: v for k, v in _L1_gnn_all.items() if k in ('W', 'a')}
    del _L1_gnn_all
    return {'x': x, 'adj': adj, 'L0_gnn_edge_table': _L0_gnn_in['edge_table'], 'L0_gnn_w_ih': _L0_gnn_in['w_ih'], 'L0_gnn_w_hh': _L0_gnn_in['w_hh'], 'L0_gnn_b_ih': _L0_gnn_in['b_ih'], 'L0_gnn_b_hh': _L0_gnn_in['b_hh'], 'L1_gnn_W': _L1_gnn_in['W'], 'L1_gnn_a': _L1_gnn_in['a']}

def reference(x, adj, L0_gnn_edge_table, L0_gnn_w_ih, L0_gnn_w_hh, L0_gnn_b_ih, L0_gnn_b_hh, L1_gnn_W, L1_gnn_a):
    import jax
    import jax.numpy as jnp

    def _L0_gnn_ref(node_features, adjacency_matrix, edge_table, w_ih, w_hh, b_ih, b_hh):
        import jax, jax.numpy as jnp
        import numpy as np
        N = 512
        H = 128
        n, h = node_features.shape
        T = edge_table.reshape(n, n, h)
        adj = adjacency_matrix.astype(node_features.dtype)
        agg = jnp.einsum('ij,jh,ijh->ih', adj, node_features, T)
        gi = agg @ w_ih.T + b_ih
        gh = node_features @ w_hh.T + b_hh
        ir, iz, in_ = jnp.split(gi, 3, axis=-1)
        hr, hz, hn = jnp.split(gh, 3, axis=-1)
        r = jax.nn.sigmoid(ir + hr)
        z = jax.nn.sigmoid(iz + hz)
        nn_ = jnp.tanh(in_ + r * hn)
        return (1.0 - z) * nn_ + z * node_features

    def _L1_gnn_ref(emb_mat, adj_mat, W, a):
        import jax, jax.numpy as jnp
        import numpy as np
        N = 6144
        IN_DIM = 128
        OUT_DIM = 128
        LR_SLOPE = 0.01
        NEG_INF = -9e+16
        out_dim = W.shape[0]
        e_new = emb_mat @ W.T
        a1 = a[:out_dim, :]
        a2 = a[out_dim:, :]
        source_scores = e_new @ a1
        target_scores = e_new @ a2
        e = source_scores + target_scores.T
        e = jax.nn.leaky_relu(e, negative_slope=LR_SLOPE)
        e = jnp.where(adj_mat > 0, e, NEG_INF)
        attention = jax.nn.softmax(e, axis=-1)
        e_transf = attention @ e_new
        return jax.nn.relu(e_transf)
    x = _layernorm(x + _L0_gnn_ref(x, adj, L0_gnn_edge_table, L0_gnn_w_ih, L0_gnn_w_hh, L0_gnn_b_ih, L0_gnn_b_hh), axis=-1)
    x = _layernorm(x + _L1_gnn_ref(x, adj, L1_gnn_W, L1_gnn_a), axis=-1)
    return x

_drawn_inputs = setup_inputs


def setup_inputs(seed=0):
    import zlib

    import numpy as np

    out = dict(_drawn_inputs(seed))
    spreads = {}
    factors = {'L0_gnn_b_ih': 4.982, 'L0_gnn_b_hh': 6.916}
    for name, (base, spread) in spreads.items():
        noise = np.random.default_rng([zlib.crc32(name.encode()), seed]).standard_normal(out[name].shape)
        drawn = base * np.exp(spread * noise) if base else spread * noise
        out[name] = jnp.asarray(drawn.astype(out[name].dtype))
    for name, factor in factors.items():
        out[name] = (out[name] * factor).astype(out[name].dtype)
    return out
```

```python
from contextlib import ExitStack

import concourse.bass as bass
from concourse import mybir

F32 = mybir.dt.float32
BF16 = mybir.dt.bfloat16
I32 = mybir.dt.int32
U32 = mybir.dt.uint32
ALU = mybir.AluOpType
ACT = mybir.ActivationFunctionType

P = 128
TOP = 8
HALVES = 2
FIRST = 12
CAPS = (24, 12, 8, 5)
BATCH = 4
A_BATCHES = HALVES * FIRST // BATCH
HOTS = 2
FACTS = 4
EPS = 1e-5
MASKED = -9e16
LEAST = -3e38


def resgnn_kernel(nc, x, xT, adj, adjT, T, w_ihT, w_hhT, b_ihT, b_hhT, W, WT, aT, out):
    N, H = x.shape
    TILES = N // P
    HALF = N // HALVES
    PER_HALF = FIRST // BATCH
    assert H == P and TILES == len(CAPS) and T.shape[0] == N * N
    B_ROUNDS = [(t, min(TOP, CAPS[t] - k)) for t in range(TILES) for k in range(0, CAPS[t], TOP)]
    B_BATCHES = [(r, k, min(BATCH, n - k)) for r, (_, n) in enumerate(B_ROUNDS) for k in range(0, n, BATCH)]
    NB = len(B_ROUNDS)
    B_FIRST = [min(r for r in range(NB) if B_ROUNDS[r][0] == t) for t in range(TILES)]
    B_LAST = [max(r for r in range(NB) if B_ROUNDS[r][0] == t) for t in range(TILES)]
    S_KEYS = [3 * t + B_FIRST[t] - t for t in range(TILES)]
    A_ALL = TILES * A_BATCHES
    ALL = A_ALL + len(B_BATCHES)

    def arrived(g):
        return sum(16 * (BATCH if b < A_ALL else B_BATCHES[b - A_ALL][2]) for b in range(g % A_BATCHES, g + 1, A_BATCHES))

    with ExitStack() as ctx:
        def sb(name, shape, dt=F32):
            return ctx.enter_context(nc.sbuf_tensor(name, shape, dt))

        def sem(name):
            return ctx.enter_context(nc.semaphore(name))

        def bank(name):
            return ctx.enter_context(nc.psum_tensor(name, [P, 512], F32))

        ident = sb("ident", [P, P])
        ones = sb("ones", [P, P])
        zeros = sb("zeros", [P, 512], BF16)
        node_key = sb("node_key", [P, N])
        row_off = sb("row_off", [P, TILES])
        neg_half = sb("neg_half", [P, TILES])
        gate_in = sb("gate_in", [P, 1])
        gate_out = sb("gate_out", [P, 1 + TILES])
        dve_gate = sb("dve_gate", [P, 1 + 2 * HALVES + TILES])
        x_facts = sb("x_facts", [P, TILES, H + FACTS])
        adj_j = sb("adj_j", [P, TILES, N], I32)
        adj_i = sb("adj_i", [P, TILES, N], I32)
        x_t = sb("x_t", [P, N])
        w_ih = sb("w_ih", [P, 3 * H])
        w_hh = sb("w_hh", [P, 3 * H])
        b_ih = sb("b_ih", [P, 3])
        b_hh = sb("b_hh", [P, 3])
        w_att = sb("w_att", [P, H])
        w_ext = sb("w_ext", [P, H + 1])
        a_att = sb("a_att", [P, 2])
        key = sb("key", [P, HALVES, HALF])
        top = sb("top", [P, HALVES, 2 * TOP])
        idx = sb("idx", [P, HALVES, FIRST], U32)
        rows = sb("rows", [P, A_BATCHES, BATCH, H])
        hot = sb("hot", [P, HOTS, BATCH, N])
        adj_f = sb("adj_f", [P, TILES, N])
        scratch = sb("scratch", [P, TILES, N])
        count = sb("count", [P, TILES, HALVES])
        over = sb("over", [P, TILES, HALVES])
        leaves = sb("leaves", [P, TILES])
        order_key = sb("order_key", [P, TILES])
        neg_order = sb("neg_order", [P, TILES])
        diag = sb("diag", [P, TILES, P])
        rank_sum = sb("rank_sum", [P, TILES])
        rank_key = sb("rank_key", [P, TILES])
        perm = sb("perm", [P, TILES, N])
        s_facts = sb("s_facts", [P, TILES, FACTS])
        s_adj = sb("s_adj", [P, TILES, N])
        s_key = sb("s_key", [P, TILES, N])
        s_top = sb("s_top", [P, NB, TOP])
        s_row = sb("s_row", [P, NB, TOP], U32)
        left_f = sb("left_f", [P, TILES])
        left = sb("left", [P, TILES], I32)
        c_top = sb("c_top", [P, TOP])
        c_idx = sb("c_idx", [P, TOP], U32)
        b_rz = sb("b_rz", [P, 2])
        b_hn = sb("b_hn", [P, 1])
        agg = sb("agg", [P, N])
        hn_half = sb("hn_half", [P, N])
        th_r = sb("th_r", [P, N])
        th_z = sb("th_z", [P, N])
        n_in = sb("n_in", [P, N])
        n_gate = sb("n_gate", [P, N])
        x_part = sb("x_part", [P, N])
        n_part = sb("n_part", [P, N])
        y_t = sb("y_t", [P, N])
        stats = sb("stats", [P, TILES, 6])
        moments = sb("moments", [P, TILES, 2])
        var_eps = sb("var_eps", [P, TILES])
        rstd = sb("rstd", [P, TILES])
        shift = sb("shift", [P, TILES])
        stats2 = sb("stats2", [P, TILES, 6])
        moments2 = sb("moments2", [P, TILES, 2])
        var_eps2 = sb("var_eps2", [P, TILES])
        rstd2 = sb("rstd2", [P, TILES])
        x1 = sb("x1", [P, TILES, H])
        x1_t = sb("x1_t", [P, N])
        att2 = sb("att2", [P, 1])
        att2_all = sb("att2_all", [P, P])
        bound = sb("bound", [P, TILES, N])
        e_ext = sb("e_ext", [P, TILES, H + 1])
        score = sb("score", [P, TILES, N])
        leaky = sb("leaky", [P, TILES, N])
        masked = sb("masked", [P, TILES, N])
        top_score = sb("top_score", [P, TILES])
        neg_top = sb("neg_top", [P, TILES])
        prob = sb("prob", [P, TILES, N])
        prob_sum = sb("prob_sum", [P, TILES])
        inv_sum = sb("inv_sum", [P, TILES])
        prob_t = sb("prob_t", [P, TILES, TILES, P])
        relu = sb("relu", [P, TILES, H])
        y2 = sb("y2", [P, TILES, H])
        out_sb = sb("out_sb", [P, TILES, H])

        ps_agg, ps_key, ps_x, ps_sx, ps_a, ps_b, ps_r, ps_z = (
            bank(f"ps_{n}") for n in ("agg", "key", "x", "sx", "a", "b", "r", "z"))
        SORTED_BANKS = (ps_sx, ps_b)
        ps_n = ps_a
        Y_BANKS = (ps_b, ps_sx)
        X1_BANKS = (ps_key, ps_x)
        E_BANKS = (ps_b, ps_sx)
        ps_t = ps_z
        PROB_BANKS = (ps_key, ps_x, ps_r, ps_a)
        OUT_BANKS = (ps_agg, ps_b, ps_sx, ps_z)

        adj_in = [sem(f"adj_in{c}") for c in range(TILES)]
        x_in, adj_i_in, gru_in, att_in = (sem(n) for n in ("x_in", "adj_i_in", "gru_in", "att_in"))
        key_made, consts_ready, ident_zero, gate_set = (
            sem(n) for n in ("key_made", "consts_ready", "ident_zero", "gate_set"))
        key_in_psum, x_in_psum = sem("key_in_psum"), sem("x_in_psum")
        key_ready, top_ready, idx_ready, pool_gated = (
            sem(n) for n in ("key_ready", "top_ready", "idx_ready", "pool_gated"))
        gathered = [sem(f"gathered{b}") for b in range(A_BATCHES)]
        made = sem("made")
        hot_free = sem("hot_free")
        sized, counted, over_ready, leaves_ready, order_ready, neg_order_ready = (
            sem(n) for n in ("sized", "counted", "over_ready", "leaves_ready", "order_ready", "neg_order_ready"))
        diag_ready, order_spread, ranked, rank_key_ready, perm_ready = (
            sem(n) for n in ("diag_ready", "order_spread", "ranked", "rank_key_ready", "perm_ready"))
        adj_f_ready, facts_ready, x_sorted, adj_sorted = (
            sem(n) for n in ("adj_f_ready", "facts_ready", "x_sorted", "adj_sorted"))
        s_facts_ready, s_adj_ready, left_f_ready, left_ready = (
            sem(n) for n in ("s_facts_ready", "s_adj_ready", "left_f_ready", "left_ready"))
        s_key_ready, s_top_ready, s_row_ready = (sem(n) for n in ("s_key_ready", "s_top_ready", "s_row_ready"))
        c_key_ready, c_top_ready, c_idx_ready, c_gathered, c_made, c_left, c_pool_gated, c_dve_gated = (
            [sem(f"{n}{t}") for t in range(TILES)]
            for n in ("c_key_ready", "c_top_ready", "c_idx_ready", "c_gathered", "c_made", "c_left",
                      "c_pool_gated", "c_dve_gated"))
        bias_sum, bias_ready, hn_done, hn_ready, agg_done, agg_copied, gates_done = (
            sem(n) for n in ("bias_sum", "bias_ready", "hn_done", "hn_ready", "agg_done", "agg_copied", "gates_done"))
        tanh_r, tanh_z, r_hn, n_sum, n_ready, x_part_ready, one_z_ready, n_part_ready, y_ready = (
            sem(n) for n in ("tanh_r", "tanh_z", "r_hn", "n_sum", "n_ready", "x_part_ready", "one_z_ready",
                             "n_part_ready", "y_ready"))
        y_turned, stats_ready, moments_ready, var_ready, rstd_ready, shift_ready = (
            sem(n) for n in ("y_turned", "stats_ready", "moments_ready", "var_ready", "rstd_ready", "shift_ready"))
        x1_low, x1_high, x1_turned, x1_t_low, x1_t_high = (
            sem(n) for n in ("x1_low", "x1_high", "x1_turned", "x1_t_low", "x1_t_high"))
        att_done, att2_ready, w_ext_ready, att_all_ready, bound_ready = (
            sem(n) for n in ("att_done", "att2_ready", "w_ext_ready", "att_all_ready", "bound_ready"))
        e_done, e_low, e_high, target_done, score_ready, leaky_ready, top_score_ready, neg_top_ready = (
            sem(n) for n in ("e_done", "e_low", "e_high", "target_done", "score_ready", "leaky_ready",
                             "top_score_ready", "neg_top_ready"))
        prob_ready, prob_turned, prob_t_low, prob_t_high, inv_ready, mixed, relu_ready = (
            sem(n) for n in ("prob_ready", "prob_turned", "prob_t_low", "prob_t_high", "inv_ready", "mixed",
                             "relu_ready"))
        y2_ready, stats2_ready, moments2_ready, var2_ready, rstd2_ready, out_ready, stored = (
            sem(n) for n in ("y2_ready", "stats2_ready", "moments2_ready", "var2_ready", "rstd2_ready",
                             "out_ready", "stored"))
        CONSTS = 5

        def sorted_x(t, n=H, to=0):
            return SORTED_BANKS[t // 2][:, (t % 2) * (H + FACTS) + to:(t % 2) * (H + FACTS) + to + n]

        def y_rows(t):
            return Y_BANKS[t // 2][:, (t % 2) * P:(t % 2 + 1) * P]

        block = ctx.enter_context(nc.Block())

        @block.sync
        def _(sp):
            adjT_v = adjT.rearrange("(p c) i -> p c i", c=TILES)
            for c in range(TILES):
                sp.dma_start(adj_j[:, c, :], adjT_v[:, c, :]).then_inc(adj_in[c], 16)
                if c == 0:
                    sp.dma_start(x_facts[:, :, 0:H], x.rearrange("(p c) h -> p c h", c=TILES)).then_inc(x_in, 16)
            for to, of in ((x_t, xT), (w_ih, w_ihT), (w_hh, w_hhT), (b_ih, b_ihT), (b_hh, b_hhT)):
                sp.dma_start(to[:, :], of).then_inc(gru_in, 16)
            for to, of in ((w_att[:, :], W), (w_ext[:, 0:H], WT), (a_att[:, :], aT)):
                sp.dma_start(to, of).then_inc(att_in, 16)
            sp.dma_start(adj_i[:, :, :], adj.rearrange("(c p) j -> p c j", p=P)).then_inc(adj_i_in, 16)
            out_v = out.rearrange("(c p) h -> c p h", p=P)
            for t in range(TILES):
                sp.wait_ge(out_ready, t + 1)
                sp.dma_start(out_v[t], out_sb[:, t, :]).then_inc(stored, 16)
            sp.wait_ge(stored, 16 * TILES)

        @block.gpsimd
        def _(pool):
            pool.iota(node_key[:, :], [[N, N]], base=N, channel_multiplier=0,
                      allow_small_or_imprecise_dtypes=True).then_inc(key_made, 1)
            pool.iota(row_off[:, :], [[1, TILES]], base=-N, channel_multiplier=TILES,
                      allow_small_or_imprecise_dtypes=True).then_inc(key_made, 1)
            pool.memset(ident[:, :], 0.0).then_inc(ident_zero, 1)
            pool.memset(ones[:, :], 1.0).then_inc(consts_ready, 1)
            pool.memset(zeros[:, :], 0.0).then_inc(consts_ready, 1)
            pool.memset(neg_half[:, :], -0.5).then_inc(consts_ready, 1)
            pool.memset(gate_in[:, :], 0.0).then_inc(consts_ready, 1)
            pool.memset(gate_out[:, :], 0.0).then_inc(pool_gated, 1)
            pool.wait_ge(ident_zero, 1)
            pool.affine_select(out=ident[:, :], in_=ident[:, :], compare_op=ALU.not_equal, fill=1.0, base=0,
                               pattern=[[-1, P]], channel_multiplier=1).then_inc(consts_ready, 1)

            def gate(passed, before, place=0):
                pool.wait_ge(passed, before)
                return pool.tensor_tensor(gate_out[:, place:place + 1], gate_in[:, :], gate_in[:, :], ALU.mult)

            def gather(to, at):
                return pool.indirect_dma_start(to, None, T, bass.IndirectOffsetOnAxis(ap=at, axis=0))

            def gather_a(h, first, last):
                for m in range(first, last):
                    b = h * PER_HALF + m // BATCH
                    gather(rows[:, b, m % BATCH, :], idx[:, h, m:m + 1]).then_inc(gathered[b], 16)

            for h in range(HALVES):
                pool.wait_ge(idx_ready, 2 * h + 1)
                gather_a(h, 0, TOP)
                pool.wait_ge(idx_ready, 2 * h + 2)
                gather_a(h, TOP, FIRST)
            pool.wait_ge(consts_ready, CONSTS)
            with pool.Fori(0, TILES - 1) as c:
                for h in range(HALVES):
                    pool.wait_ge(idx_ready, c * (2 * HALVES) + (2 * HALVES + 2 * h + 2))
                    pool.wait_ge(hot_free, c * A_BATCHES + (PER_HALF * (h + 1) + HOTS))
                    gate(pool_gated, c * HALVES + (h + 1)).then_inc(pool_gated, 1)
                    gather_a(h, 0, FIRST)
            pool.wait_ge(left_ready, 1)
            n_left = [pool.value_load(left[0:1, t:t + 1], min_val=0, max_val=N) for t in range(TILES)]
            for j, (r, first, n) in enumerate(B_BATCHES):
                g = A_ALL + j
                pool.wait_ge(s_row_ready, r + 1)
                pool.wait_ge(hot_free, HOTS + g - A_BATCHES + 1)
                for k in range(n):
                    gather(rows[:, g % A_BATCHES, k, :], s_row[:, r, first + k:first + k + 1]).then_inc(
                        gathered[g % A_BATCHES], 16)
            for t in range(TILES):
                with pool.If(n_left[t] > 0):
                    pool.memset(gate_out[:, 1 + t:2 + t], 0.0).then_inc(c_pool_gated[t], TOP)
                    with pool.Fori(0, n_left[t], TOP) as i:
                        pool.wait_ge(c_idx_ready[t], i + TOP)
                        gate(c_pool_gated[t], i + TOP, 1 + t).then_inc(c_pool_gated[t], TOP)
                        for k in range(TOP):
                            gather(rows[:, k // BATCH, k % BATCH, :], c_idx[:, k:k + 1]).then_inc(c_gathered[t], 16)
            pool.wait_ge(tanh_z, 1)
            pool.tensor_scalar(n_part[:, :], th_z[:, :], -1.0, 1.0, ALU.mult, ALU.add).then_inc(one_z_ready, 1)
            pool.wait_ge(var_ready, 1)
            pool.tensor_tensor(rstd[:, :], var_eps[:, :], neg_half[:, :], ALU.pow).then_inc(rstd_ready, 1)
            for u in range(0, TILES, 2):
                pool.wait_ge(var2_ready, u // 2 + 1)
                pool.tensor_tensor(rstd2[:, u:u + 2], var_eps2[:, u:u + 2], neg_half[:, u:u + 2],
                                   ALU.pow).then_inc(rstd2_ready, 1)

        @block.vector
        def _(dve):
            def gate(place):
                return dve.tensor_copy(dve_gate[:, 1 + place:2 + place], dve_gate[:, 0:1])

            def times_key(to, adjacency, keys):
                return dve.scalar_tensor_tensor(out=to, in0=adjacency, scalar=0.0, in1=keys,
                                                op0=ALU.not_equal, op1=ALU.mult)

            def row_index(to, of, offset):
                return dve.tensor_scalar(to, of, offset, 0.0, ALU.add, ALU.max)

            def find_a(c, h):
                half = slice(h * HALF, (h + 1) * HALF)
                done = c * (2 * HALVES) + 2 * h
                off = row_off[:, bass.ds(c, 1)]
                times_key(key[:, h, :], adj_j[:, c, half], node_key[:, half]).then_inc(key_ready, 1)
                dve.wait_ge(key_ready, done + 1)
                gate(2 * h)
                dve.max(top[:, h, 0:TOP], key[:, h, :]).then_inc(top_ready, 1)
                dve.wait_ge(top_ready, done + 1)
                row_index(idx[:, h, 0:TOP], top[:, h, 0:TOP], off).then_inc(idx_ready, 1)
                dve.match_replace(key[:, h, :], top[:, h, 0:TOP], key[:, h, :], 0.0).then_inc(key_ready, 1)
                dve.wait_ge(key_ready, done + 2)
                gate(2 * h + 1)
                dve.max(top[:, h, TOP:2 * TOP], key[:, h, :]).then_inc(top_ready, 1)
                dve.wait_ge(top_ready, done + 2)
                row_index(idx[:, h, TOP:FIRST], top[:, h, TOP:FIRST], off).then_inc(idx_ready, 1)
                dve.tensor_copy(x_facts[:, bass.ds(c, 1), H + 2 + h:H + 3 + h].rearrange("p c f -> p (c f)"),
                                top[:, h, FIRST - 1:FIRST]).then_inc(facts_ready, 1)

            def times_x(batch, n, features):
                return dve.tensor_tensor(rows[:, batch, 0:n, :], rows[:, batch, 0:n, :],
                                         features.unsqueeze(1).to_broadcast([P, n, H]), ALU.mult)

            def edges_a(c, b):
                h, q = b // PER_HALF, b % PER_HALF
                half = slice(h * HALF, (h + 1) * HALF)
                dve.wait_ge(hot_free, c * A_BATCHES + (b + 1))
                for k in range(BATCH):
                    m = q * BATCH + k
                    dve.scalar_tensor_tensor(out=hot[:, b % HOTS, k, 0:HALF], in0=ps_key[:, half],
                                             scalar=top[:, h, m:m + 1], in1=adj_j[:, c, half],
                                             op0=ALU.is_equal, op1=ALU.mult)
                dve.wait_ge(gathered[b], c * (16 * BATCH) + 16 * BATCH)
                times_x(b, BATCH, ps_x[:, bass.ds(c * H, H)]).then_inc(made, 1)

            dve.memset(dve_gate[:, :], 0.0).then_inc(gate_set, 1)
            dve.wait_ge(gate_set, 1)
            dve.wait_ge(key_made, 2)
            dve.wait_ge(adj_in[0], 16)
            find_a(0, 0)
            find_a(0, 1)
            dve.wait_ge(counted, TILES * HALVES)
            dve.tensor_scalar(over[:, :, :], count[:, :, :], -float(FIRST), 0.0, ALU.add, ALU.max).then_inc(
                over_ready, 1)
            dve.wait_ge(over_ready, 1)
            dve.tensor_tensor(leaves[:, :], over[:, :, 0], over[:, :, 1], ALU.add).then_inc(leaves_ready, 1)
            dve.wait_ge(leaves_ready, 1)
            dve.scalar_tensor_tensor(out=order_key[:, :], in0=leaves[:, :], scalar=float(N), in1=row_off[:, :],
                                     op0=ALU.mult, op1=ALU.add).then_inc(order_ready, 1)
            dve.tensor_copy(x_facts[:, :, H], row_off[:, :]).then_inc(facts_ready, 1)
            dve.tensor_copy(x_facts[:, :, H + 1], leaves[:, :]).then_inc(facts_ready, 1)
            dve.wait_ge(order_ready, 1)
            dve.tensor_scalar(neg_order[:, :], order_key[:, :], -1.0, None, ALU.mult).then_inc(neg_order_ready, 1)

            dve.wait_ge(key_in_psum, 1)
            dve.wait_ge(ranked, TILES)
            dve.tensor_scalar(rank_key[:, :], rank_sum[:, :], N / 2.0, N * (N - 1) / 2.0 + N, ALU.mult,
                              ALU.add).then_inc(rank_key_ready, 1)
            dve.wait_ge(rank_key_ready, 1)
            for c in range(TILES):
                dve.tensor_scalar(perm[:, c, :], ps_key[:, :], rank_key[:, c:c + 1], None,
                                  ALU.is_equal).then_inc(perm_ready, 1)
            dve.wait_ge(x_in_psum, 1)
            for c in range(1, TILES):
                dve.wait_ge(adj_in[c], 16)
            with dve.Fori(0, TILES - 1) as c:
                for h in range(HALVES):
                    for b in range(h * PER_HALF, (h + 1) * PER_HALF):
                        edges_a(c, b)
                    find_a(c + 1, h)

            def find_b(r):
                t, n = B_ROUNDS[r]
                base = S_KEYS[t]
                if r == B_FIRST[t]:
                    dve.wait_ge(s_adj_ready, t + 1)
                    for h in range(HALVES):
                        half = slice(h * HALF, (h + 1) * HALF)
                        dve.scalar_tensor_tensor(out=s_key[:, t, half], in0=node_key[:, half],
                                                 scalar=s_facts[:, t, 2 + h:3 + h], in1=s_adj[:, t, half],
                                                 op0=ALU.is_lt, op1=ALU.mult).then_inc(s_key_ready, 1)
                    dve.wait_ge(s_key_ready, base + 2)
                    times_key(s_key[:, t, :], s_key[:, t, :], node_key[:, :]).then_inc(s_key_ready, 1)
                dve.wait_ge(s_key_ready, base + 3 + (r - B_FIRST[t]))
                dve.max(s_top[:, r, :], s_key[:, t, :]).then_inc(s_top_ready, 1)
                dve.wait_ge(s_top_ready, r + 1)
                row_index(s_row[:, r, :], s_top[:, r, :], s_facts[:, t, 0:1]).then_inc(s_row_ready, 1)
                if r != B_LAST[t]:
                    dve.match_replace(s_key[:, t, :], s_top[:, r, :], s_key[:, t, :], 0.0).then_inc(s_key_ready, 1)

            def edges_b(r):
                t, _ = B_ROUNDS[r]
                for j, (of, first, n) in enumerate(B_BATCHES):
                    if of != r:
                        continue
                    g = A_ALL + j
                    dve.wait_ge(hot_free, g + 1)
                    for k in range(n):
                        dve.scalar_tensor_tensor(out=hot[:, g % HOTS, k, :], in0=ps_key[:, :],
                                                 scalar=s_top[:, r, first + k:first + k + 1], in1=s_adj[:, t, :],
                                                 op0=ALU.is_equal, op1=ALU.mult)
                    dve.wait_ge(gathered[g % A_BATCHES], arrived(g))
                    times_x(g % A_BATCHES, n, sorted_x(t)).then_inc(made, 1)

            for b in range(A_BATCHES):
                edges_a(TILES - 1, b)
                if b == 1:
                    dve.wait_ge(x_sorted, 1)
                    for t in range(TILES):
                        dve.tensor_copy(s_facts[:, t, :], sorted_x(t, FACTS, H)).then_inc(s_facts_ready, 1)
                    dve.wait_ge(s_facts_ready, TILES)
                    for t in range(TILES):
                        dve.tensor_scalar(left_f[:, t:t + 1], s_facts[:, t, 1:2], -float(CAPS[t]), 0.0, ALU.add,
                                          ALU.max).then_inc(left_f_ready, 1)
                    dve.wait_ge(left_f_ready, TILES)
                    dve.tensor_copy(left[:, :], left_f[:, :]).then_inc(left_ready, 1)
                if b >= 1 and b - 1 < B_FIRST[2]:
                    find_b(b - 1)
            found = min(A_BATCHES - 1, B_FIRST[2])
            dve.wait_ge(left_ready, 1)
            n_left = [dve.value_load(left[0:1, t:t + 1], min_val=0, max_val=N) for t in range(TILES)]
            for r in range(NB):
                edges_b(r)
                if found < NB:
                    find_b(found)
                    found += 1

            for t in range(TILES):
                with dve.If(n_left[t] > 0):
                    dve.memset(dve_gate[:, 1 + 2 * HALVES + t:2 + 2 * HALVES + t], 0.0).then_inc(c_dve_gated[t], TOP)
                    for h in range(HALVES):
                        half = slice(h * HALF, (h + 1) * HALF)
                        dve.scalar_tensor_tensor(out=s_key[:, t, half], in0=node_key[:, half],
                                                 scalar=s_facts[:, t, 2 + h:3 + h], in1=s_adj[:, t, half],
                                                 op0=ALU.is_lt, op1=ALU.mult).then_inc(c_key_ready[t], 1)
                    final = B_ROUNDS[B_LAST[t]][1] - 1
                    dve.wait_ge(c_key_ready[t], 2)
                    dve.scalar_tensor_tensor(out=s_key[:, t, :], in0=node_key[:, :],
                                             scalar=s_top[:, B_LAST[t], final:final + 1], in1=s_key[:, t, :],
                                             op0=ALU.is_lt, op1=ALU.mult).then_inc(c_key_ready[t], 1)
                    dve.wait_ge(c_key_ready[t], 3)
                    times_key(s_key[:, t, :], s_key[:, t, :], node_key[:, :]).then_inc(c_key_ready[t], TOP - 3)
                    dve.wait_ge(hot_free, ALL + HOTS)
                    with dve.Fori(0, n_left[t], TOP) as i:
                        dve.wait_ge(c_key_ready[t], i + TOP)
                        dve.wait_ge(c_dve_gated[t], i + TOP)
                        gate(2 * HALVES + t).then_inc(c_dve_gated[t], TOP)
                        dve.max(c_top[:, :], s_key[:, t, :]).then_inc(c_top_ready[t], TOP)
                        dve.wait_ge(c_top_ready[t], i + TOP)
                        row_index(c_idx[:, :], c_top[:, :], s_facts[:, t, 0:1]).then_inc(c_idx_ready[t], TOP)
                        dve.match_replace(s_key[:, t, :], c_top[:, :], s_key[:, t, :], 0.0).then_inc(
                            c_key_ready[t], TOP)
                        for k in range(TOP):
                            dve.scalar_tensor_tensor(out=hot[:, k // BATCH, k % BATCH, :], in0=ps_key[:, :],
                                                     scalar=c_top[:, k:k + 1], in1=s_adj[:, t, :],
                                                     op0=ALU.is_equal, op1=ALU.mult)
                        dve.wait_ge(c_gathered[t], i * 16 + 16 * TOP)
                        for b in range(TOP // BATCH):
                            times_x(b, BATCH, sorted_x(t)).then_inc(c_made[t], TOP // HOTS)
                        dve.wait_ge(c_left[t], i + TOP)

            dve.wait_ge(tanh_r, 1)
            dve.wait_ge(hn_ready, 1)
            dve.scalar_tensor_tensor(out=n_in[:, :], in0=th_r[:, :], scalar=1.0, in1=hn_half[:, :],
                                     op0=ALU.add, op1=ALU.mult).then_inc(r_hn, 1)
            dve.wait_ge(r_hn, 1)
            dve.wait_ge(gates_done, 2)
            for h in range(HALVES):
                half = slice(h * HALF, (h + 1) * HALF)
                dve.tensor_tensor(n_in[:, half], n_in[:, half], ps_n[:, half], ALU.add).then_inc(n_sum, 1)
            dve.wait_ge(tanh_z, 1)
            dve.scalar_tensor_tensor(out=x_part[:, :], in0=th_z[:, :], scalar=3.0, in1=x_t[:, :],
                                     op0=ALU.add, op1=ALU.mult).then_inc(x_part_ready, 1)
            dve.wait_ge(one_z_ready, 1)
            for h in range(HALVES):
                half = slice(h * HALF, (h + 1) * HALF)
                dve.wait_ge(n_ready, h + 1)
                dve.tensor_tensor(n_gate[:, half], n_gate[:, half], n_part[:, half], ALU.mult).then_inc(
                    n_part_ready, 1)
                dve.wait_ge(x_part_ready, 1)
                dve.wait_ge(n_part_ready, h + 1)
                dve.tensor_tensor(y_t[:, half], n_gate[:, half], x_part[:, half], ALU.add).then_inc(y_ready, 1)

            for t in range(TILES):
                dve.wait_ge(y_turned, t // 2 + 1)
                dve.bn_stats(stats[:, t, :], y_rows(t)).then_inc(stats_ready, 1)
            for t in range(TILES):
                dve.wait_ge(stats_ready, t + 1)
                dve.bn_aggr(moments[:, t, :], stats[:, t, :]).then_inc(moments_ready, 1)
            dve.wait_ge(moments_ready, TILES)
            dve.tensor_scalar(var_eps[:, :], moments[:, :, 1], 4 * EPS, None, ALU.add).then_inc(var_ready, 1)
            dve.wait_ge(rstd_ready, 1)
            dve.scalar_tensor_tensor(out=shift[:, 2:4], in0=moments[:, 2:4, 0], scalar=-1.0, in1=rstd[:, 2:4],
                                     op0=ALU.mult, op1=ALU.mult).then_inc(shift_ready, 1)
            for t in range(2):
                dve.tensor_scalar(x1[:, t, :], y_rows(t), moments[:, t, 0:1], rstd[:, t:t + 1],
                                  ALU.subtract, ALU.mult).then_inc(x1_low, 1)
            dve.wait_ge(x1_turned, 1)
            dve.tensor_copy(x1_t[:, 0:2 * P], X1_BANKS[0][:, 0:2 * P]).then_inc(x1_t_low, 1)
            dve.wait_ge(e_done, 1)
            dve.tensor_copy(e_ext[:, 0:2, :].rearrange("p t h -> p (t h)"),
                            E_BANKS[0][:, 0:2 * (H + 1)]).then_inc(e_low, 1)

            for t in range(TILES):
                dve.wait_ge(score_ready, t + 1)
                dve.scalar_tensor_tensor(out=leaky[:, t, :], in0=score[:, t, :], scalar=0.01, in1=score[:, t, :],
                                         op0=ALU.mult, op1=ALU.max).then_inc(leaky_ready, 1)
                dve.wait_ge(leaky_ready, t + 1)
                dve.wait_ge(bound_ready, 3 * TILES)
                dve.tensor_tensor_reduce(out=masked[:, t, :], in0=leaky[:, t, :], in1=bound[:, t, :], scale=1.0,
                                         scalar=LEAST, op0=ALU.add, op1=ALU.max,
                                         accum_out=top_score[:, t:t + 1]).then_inc(top_score_ready, 1)
                dve.wait_ge(top_score_ready, t + 1)
                dve.tensor_scalar(neg_top[:, t:t + 1], top_score[:, t:t + 1], -1.0, None,
                                  ALU.mult).then_inc(neg_top_ready, 1)

            def residual(t):
                dve.wait_ge(relu_ready, t + 1)
                dve.tensor_tensor(y2[:, t, :], relu[:, t, :], x1[:, t, :], ALU.add).then_inc(y2_ready, 1)
                dve.wait_ge(y2_ready, t + 1)
                dve.bn_stats(stats2[:, t, :], y2[:, t, :]).then_inc(stats2_ready, 1)
                dve.wait_ge(stats2_ready, t + 1)
                dve.bn_aggr(moments2[:, t, :], stats2[:, t, :]).then_inc(moments2_ready, 1)

            def variances(u):
                dve.wait_ge(moments2_ready, u + 2)
                dve.tensor_scalar(var_eps2[:, u:u + 2], moments2[:, u:u + 2, 1], EPS, None, ALU.add).then_inc(
                    var2_ready, 1)

            def normalise(u):
                dve.wait_ge(rstd2_ready, u // 2 + 1)
                for t in range(u, u + 2):
                    dve.tensor_scalar(out_sb[:, t, :], y2[:, t, :], moments2[:, t, 0:1], rstd2[:, t:t + 1],
                                      ALU.subtract, ALU.mult).then_inc(out_ready, 1)

            for u in range(2):
                dve.wait_ge(prob_ready, 2 * u + 2)
                dve.reciprocal(inv_sum[:, 2 * u:2 * u + 2], prob_sum[:, 2 * u:2 * u + 2]).then_inc(inv_ready, 1)
                dve.wait_ge(prob_turned, u + 3)
                dve.tensor_copy(prob_t[:, u + 2, :, :].rearrange("p c i -> p (c i)"),
                                PROB_BANKS[u + 2][:, :]).then_inc(prob_t_high, 1)
            residual(0)
            residual(1)
            variances(0)
            residual(2)
            normalise(0)
            residual(3)
            variances(2)
            normalise(2)

        @block.scalar
        def _(act):
            act.wait_ge(key_made, 1)
            act.copy(ps_key[:, :], node_key[:, :]).then_inc(key_in_psum, 1)
            for c in range(TILES):
                act.wait_ge(adj_in[c], 16)
                act.activation(scratch[:, c, :], adj_j[:, c, :], ACT.Abs).then_inc(sized, 1)
                act.wait_ge(sized, c + 1)
                for h in range(HALVES):
                    act.activation(adj_f[:, c, h * HALF:(h + 1) * HALF], scratch[:, c, h * HALF:(h + 1) * HALF],
                                   ACT.Sign, accum_out=count[:, c, h:h + 1]).then_inc(counted, 1)
                if c == 0:
                    act.wait_ge(x_in, 16)
                    act.copy(ps_x[:, :].rearrange("p (c h) -> p c h", h=H), x_facts[:, :, 0:H]).then_inc(x_in_psum, 1)
            act.wait_ge(consts_ready, CONSTS)
            act.wait_ge(order_ready, 1)
            for c in range(TILES):
                act.mul(diag[:, c, :], ident[:, :], order_key[:, c:c + 1]).then_inc(diag_ready, 1)
            act.wait_ge(neg_order_ready, 1)
            act.wait_ge(order_spread, 1)
            act.wait_ge(counted, TILES * HALVES)
            for c in range(TILES):
                act.activation(scratch[:, c, :], ps_a[:, :], ACT.Sign, bias=neg_order[:, c:c + 1],
                               accum_out=rank_sum[:, c:c + 1]).then_inc(ranked, 1)
            for c in range(TILES):
                act.copy(adj_f[:, c, :], adj_j[:, c, :]).then_inc(adj_f_ready, 1)
            act.wait_ge(gru_in, 16 * 5)
            for g in range(2):
                act.activation(b_rz[:, g:g + 1], b_ih[:, g:g + 1], ACT.Identity,
                               bias=b_hh[:, g:g + 1]).then_inc(bias_sum, 1)
            act.wait_ge(bias_sum, 2)
            act.mul(b_rz[:, :], b_rz[:, :], 0.5).then_inc(bias_ready, 1)
            act.mul(b_hn[:, :], b_hh[:, 2:3], 0.5).then_inc(bias_ready, 1)
            act.wait_ge(hn_done, 1)
            act.wait_ge(bias_ready, 2)
            act.activation(hn_half[:, :], ps_z[:, :], ACT.Identity, bias=b_hn[:, 0:1], scale=0.5).then_inc(hn_ready, 1)
            act.wait_ge(att_in, 16 * 3)
            act.wait_ge(att_done, 1)
            act.copy(w_ext[:, H:H + 1], ps_b[:, 0:1]).then_inc(w_ext_ready, 1)
            act.copy(att2[:, :], ps_b[:, 1:2]).then_inc(att2_ready, 1)
            act.wait_ge(att2_ready, 1)
            act.mul(att2_all[:, :], ones[:, :], att2[:, 0:1]).then_inc(att_all_ready, 1)
            for t in range(TILES):
                act.wait_ge(adj_sorted, t + 1)
                act.copy(s_adj[:, t, :], (ps_a, ps_r)[t % 2][:, :]).then_inc(s_adj_ready, 1)
            act.wait_ge(adj_i_in, 16)
            for t in range(TILES):
                act.activation(bound[:, t, :], adj_i[:, t, :], ACT.Relu).then_inc(bound_ready, 1)
                act.wait_ge(bound_ready, 3 * t + 1)
                act.activation(bound[:, t, :], bound[:, t, :], ACT.Sign).then_inc(bound_ready, 1)
                act.wait_ge(bound_ready, 3 * t + 2)
                act.activation(bound[:, t, :], bound[:, t, :], ACT.Copy, scale=-MASKED,
                               bias=MASKED).then_inc(bound_ready, 1)
            act.wait_ge(agg_done, 1)
            act.copy(agg[:, :], ps_agg[:, :]).then_inc(agg_copied, 1)
            act.wait_ge(gates_done, 1)
            act.activation(th_r[:, :], ps_r[:, :], ACT.Tanh, bias=b_rz[:, 0:1], scale=0.5).then_inc(tanh_r, 1)
            act.wait_ge(gates_done, 3)
            act.activation(th_z[:, :], ps_z[:, :], ACT.Tanh, bias=b_rz[:, 1:2], scale=0.5).then_inc(tanh_z, 1)
            for h in range(HALVES):
                half = slice(h * HALF, (h + 1) * HALF)
                act.wait_ge(n_sum, h + 1)
                act.activation(n_gate[:, half], n_in[:, half], ACT.Tanh, bias=b_ih[:, 2:3]).then_inc(n_ready, 1)
            act.wait_ge(shift_ready, 1)
            for t in range(2, TILES):
                act.activation(x1[:, t, :], y_rows(t), ACT.Identity, bias=shift[:, t:t + 1],
                               scale=rstd[:, t:t + 1]).then_inc(x1_high, 1)
            act.wait_ge(x1_turned, 2)
            act.copy(x1_t[:, 2 * P:4 * P], X1_BANKS[1][:, 0:2 * P]).then_inc(x1_t_high, 1)
            act.wait_ge(target_done, 1)
            act.wait_ge(e_low, 1)
            for t in range(TILES):
                if t == 2:
                    act.wait_ge(e_high, 1)
                act.activation(score[:, t, :], ps_t[:, :], ACT.Identity, bias=e_ext[:, t, H:H + 1]).then_inc(
                    score_ready, 1)
                if t == 1:
                    act.wait_ge(e_done, 2)
                    act.copy(e_ext[:, 2:4, :].rearrange("p t h -> p (t h)"),
                             E_BANKS[1][:, 0:2 * (H + 1)]).then_inc(e_high, 1)
            for t in range(TILES):
                act.wait_ge(neg_top_ready, t + 1)
                act.activation(prob[:, t, :], masked[:, t, :], ACT.Exp, bias=neg_top[:, t:t + 1],
                               accum_out=prob_sum[:, t:t + 1]).then_inc(prob_ready, 1)
                if t >= 1 and t < 3:
                    act.wait_ge(prob_turned, t)
                    act.copy(prob_t[:, t - 1, :, :].rearrange("p c i -> p (c i)"),
                             PROB_BANKS[t - 1][:, :]).then_inc(prob_t_low, 1)
            for t in range(TILES):
                act.wait_ge(mixed, t + 1)
                act.wait_ge(inv_ready, t // 2 + 1)
                act.activation(relu[:, t, :], OUT_BANKS[t][:, 0:H], ACT.Relu,
                               scale=inv_sum[:, t:t + 1]).then_inc(relu_ready, 1)

        @block.tensor
        def _(pe):
            pe.wait_ge(consts_ready, CONSTS)
            pe.matmul(ps_agg[:, :], zeros[:, 0:P], zeros[:, :], start=True, stop=False,
                      skip_group_check=True).then_inc(hot_free, HOTS)
            pe.wait_ge(gru_in, 16 * 5)
            pe.matmul(ps_z[:, :], w_hh[:, 2 * H:3 * H], x_t[:, :], start=True, stop=True).then_inc(hn_done, 1)
            pe.wait_ge(att_in, 16 * 3)
            pe.matmul(ps_b[:, 0:2], w_att[:, :], a_att[:, :], start=True, stop=True).then_inc(att_done, 1)
            for c in range(TILES):
                pe.wait_ge(diag_ready, c + 1)
                spread = pe.matmul(ps_a[:, c * P:(c + 1) * P], ones[:, :], diag[:, c, :], start=True, stop=True)
            spread.then_inc(order_spread, 1)

            def add_batch_a(b, ready):
                h = b // PER_HALF
                pe.wait_ge(made, ready)
                for k in range(BATCH):
                    last = pe.matmul(ps_agg[:, h * HALF:(h + 1) * HALF], rows[:, b, k, :],
                                     hot[:, b % HOTS, k, 0:HALF], start=False, stop=False, skip_group_check=True)
                last.then_inc(hot_free, 1)

            def sort_adj(t, part):
                if part == 0 and t >= 2:
                    pe.wait_ge(s_adj_ready, t - 1)
                for c in range(part * TILES // 2, (part + 1) * TILES // 2):
                    last = pe.matmul((ps_a, ps_r)[t % 2][:, :], perm[:, c, t * P:(t + 1) * P], adj_f[:, c, :],
                                     start=(c == 0), stop=(c == TILES - 1), skip_group_check=True)
                if part == 1:
                    last.then_inc(adj_sorted, 1)

            pe.wait_ge(perm_ready, TILES)
            pe.wait_ge(ranked, TILES)
            pe.wait_ge(adj_f_ready, TILES)
            parts = [(t, part) for t in range(TILES) for part in range(2)]
            for b in range(A_BATCHES):
                sort_adj(*parts[b])
                add_batch_a(b, b + 1)
            for t, part in parts[A_BATCHES:]:
                sort_adj(t, part)
            with pe.Fori(1, TILES - 1) as c:
                for b in range(A_BATCHES):
                    add_batch_a(b, c * A_BATCHES + (b + 1))
            pe.wait_ge(facts_ready, 2 + TILES * HALVES)
            pe.wait_ge(x_in, 16)
            pe.wait_ge(att_all_ready, 1)
            for t in range(TILES):
                for c in range(TILES):
                    last = pe.matmul(sorted_x(t, H + FACTS), perm[:, c, t * P:(t + 1) * P], x_facts[:, c, :],
                                     start=(c == 0), stop=(c == TILES - 1))
            last.then_inc(x_sorted, 1)
            for b in range(A_BATCHES):
                add_batch_a(b, (TILES - 1) * A_BATCHES + b + 1)
                if b in (2, 4):
                    gate = (b - 2) // 2
                    if gate == 0:
                        pe.wait_ge(s_adj_ready, TILES)
                    else:
                        pe.wait_ge(hn_ready, 1)
                    pe.matmul((ps_r, ps_z)[gate][:, :], w_hh[:, gate * H:(gate + 1) * H], x_t[:, :], start=True,
                              stop=False, skip_group_check=True)
            pe.wait_ge(left_ready, 1)
            n_left = [pe.value_load(left[0:1, t:t + 1], min_val=0, max_val=N) for t in range(TILES)]
            for j, (r, first, n) in enumerate(B_BATCHES):
                g = A_ALL + j
                pe.wait_ge(made, g + 1)
                for k in range(n):
                    last = pe.matmul(ps_agg[:, :], rows[:, g % A_BATCHES, k, :], hot[:, g % HOTS, k, :],
                                     start=False, stop=False, skip_group_check=True)
                last.then_inc(hot_free, 1)
            for t in range(TILES):
                with pe.If(n_left[t] > 0):
                    with pe.Fori(0, n_left[t], TOP) as i:
                        for b in range(TOP // BATCH):
                            pe.wait_ge(c_made[t], i + (b + 1) * BATCH)
                            for k in range(BATCH):
                                pe.matmul(ps_agg[:, :], rows[:, b, k, :], hot[:, b, k, :], start=False, stop=False,
                                          skip_group_check=True).then_inc(c_left[t], 1)
            pe.matmul(ps_agg[:, :], zeros[:, 0:P], zeros[:, :], start=False, stop=True,
                      skip_group_check=True).then_inc(agg_done, 1)

            pe.wait_ge(agg_copied, 1)
            pe.matmul(ps_r[:, :], w_ih[:, 0:H], agg[:, :], start=False, stop=True,
                      skip_group_check=True).then_inc(gates_done, 1)
            pe.matmul(ps_n[:, :], w_ih[:, 2 * H:3 * H], agg[:, :], start=True, stop=True).then_inc(gates_done, 1)
            pe.matmul(ps_z[:, :], w_ih[:, H:2 * H], agg[:, :], start=False, stop=True,
                      skip_group_check=True).then_inc(gates_done, 1)
            for u in range(2):
                pe.wait_ge(y_ready, u + 1)
                for t in (2 * u, 2 * u + 1):
                    last = pe.transpose(y_rows(t), y_t[:, t * P:(t + 1) * P], ident[:, :])
                last.then_inc(y_turned, 1)
            for u in range(2):
                pe.wait_ge((x1_low, x1_high)[u], 2)
                for t in (2 * u, 2 * u + 1):
                    last = pe.transpose(X1_BANKS[u][:, (t % 2) * P:(t % 2 + 1) * P], x1[:, t, :], ident[:, :])
                last.then_inc(x1_turned, 1)

            pe.wait_ge(w_ext_ready, 1)
            for u in range(2):
                pe.wait_ge((x1_t_low, x1_t_high)[u], 1)
                for t in (2 * u, 2 * u + 1):
                    last = pe.matmul(E_BANKS[u][:, (t % 2) * (H + 1):(t % 2 + 1) * (H + 1)],
                                     x1_t[:, t * P:(t + 1) * P], w_ext[:, :], start=True, stop=True)
                last.then_inc(e_done, 1)
            pe.wait_ge(att_all_ready, 1)
            pe.matmul(ps_t[:, :], att2_all[:, :], x1_t[:, :], start=True, stop=True).then_inc(target_done, 1)

            def turn(t):
                pe.wait_ge(prob_ready, t + 1)
                for c in range(TILES):
                    last = pe.transpose(PROB_BANKS[t][:, c * P:(c + 1) * P], prob[:, t, c * P:(c + 1) * P],
                                        ident[:, :])
                last.then_inc(prob_turned, 1)

            def mix(t):
                pe.wait_ge((prob_t_low, prob_t_high)[t // 2], t % 2 + 1)
                for c in range(TILES):
                    last = pe.matmul(OUT_BANKS[t][:, 0:H], prob_t[:, t, c, :], e_ext[:, c, 0:H],
                                     start=(c == 0), stop=(c == TILES - 1))
                last.then_inc(mixed, 1)

            turn(0)
            turn(1)
            pe.wait_ge(e_low, 1)
            pe.wait_ge(e_high, 1)
            mix(0)
            turn(2)
            mix(1)
            turn(3)
            mix(2)
            mix(3)


def kernel(x, adj, L0_gnn_edge_table, L0_gnn_w_ih, L0_gnn_w_hh, L0_gnn_b_ih, L0_gnn_b_hh, L1_gnn_W, L1_gnn_a):
    import numpy as np
    import concourse.bacc as bacc
    from concourse.bass_utils import run_bass_kernel_spmd

    x, adj = np.asarray(x), np.asarray(adj)
    w, a = np.asarray(L1_gnn_W), np.asarray(L1_gnn_a)
    H = x.shape[1]
    laid = {
        "x": x,
        "xT": x.T,
        "adj": adj,
        "adjT": adj.T,
        "T": np.asarray(L0_gnn_edge_table),
        "w_ihT": np.asarray(L0_gnn_w_ih).T,
        "w_hhT": np.asarray(L0_gnn_w_hh).T,
        "b_ihT": np.asarray(L0_gnn_b_ih).reshape(3, H).T,
        "b_hhT": np.asarray(L0_gnn_b_hh).reshape(3, H).T,
        "W": w,
        "WT": w.T,
        "aT": a.reshape(2, H).T,
    }
    nc = bacc.Bacc("TRN2", target_bir_lowering=False, num_devices=1)
    arrays, args = {}, {}
    for name, value in laid.items():
        value = np.ascontiguousarray(value)
        arrays[f"in_{name}"] = value
        args[name] = nc.dram_tensor(f"in_{name}", value.shape, mybir.dt.from_np(value.dtype),
                                    kind="ExternalInput").ap()
    args["out"] = nc.dram_tensor("out_x", x.shape, F32, kind="ExternalOutput").ap()
    resgnn_kernel(nc, **args)
    return run_bass_kernel_spmd(nc, [arrays], core_ids=[0]).results[0]["out_x"]
```

```python
from contextlib import ExitStack

import concourse.bass as bass
from concourse import mybir

F32 = mybir.dt.float32
BF16 = mybir.dt.bfloat16
I32 = mybir.dt.int32
U32 = mybir.dt.uint32
ALU = mybir.AluOpType
ACT = mybir.ActivationFunctionType

P = 128
TOP = 8
HALVES = 2
DENSE = 40
BLOCK = 2
A_SIZES = (4, 4, 4)
FIRST = sum(A_SIZES)
CAPS = (21, 9, 6, 3)
BATCH = 4
PER_HALF = len(A_SIZES)
A_BATCHES = HALVES * PER_HALF
HOTS = 3
FACTS = 4
EPS = 1e-5
MASKED = -9e16
LEAST = -3e38
B_AHEAD = 3
WARM = (7, 3, 11, 2)


def resgnn_kernel(nc, x, xT, adj, adjT, T, w_ihT, w_hhT, b_ihT, b_hhT, W, WT, aT, out):
    N, H = x.shape
    TILES = N // P
    SPARSE = N - DENSE
    HALF = SPARSE // HALVES
    BLOCKS = DENSE // BLOCK
    FIRST_TILE = 1
    B_DENSE = BLOCKS - (TILES - FIRST_TILE) * A_BATCHES
    PER_TILE = A_BATCHES * BLOCK
    assert H == P and TILES == len(CAPS) and T.shape[0] == N * N
    B_ROUNDS = [(t, min(TOP, CAPS[t] - k)) for t in range(TILES) for k in range(0, CAPS[t], TOP)]
    B_SIZES = [BATCH] * (TILES - 2) + [BATCH // 2, 1]
    B_BATCHES = [(r, k, min(B_SIZES[t], n - k)) for r, (t, n) in enumerate(B_ROUNDS)
                 for k in range(0, n, B_SIZES[t])]
    NB = len(B_ROUNDS)
    B_FIRST = [min(r for r in range(NB) if B_ROUNDS[r][0] == t) for t in range(TILES)]
    B_LAST = [max(r for r in range(NB) if B_ROUNDS[r][0] == t) for t in range(TILES)]
    S_KEYS = [2 * t + B_FIRST[t] - t for t in range(TILES)]
    A_ALL = TILES * A_BATCHES
    ALL = A_ALL + len(B_BATCHES)

    def arrived(g):
        return sum(16 * (A_SIZES[b % PER_HALF] if b < A_ALL else B_BATCHES[b - A_ALL][2])
                   for b in range(g % A_BATCHES, g + 1, A_BATCHES))

    with ExitStack() as ctx:
        def sb(name, shape, dt=F32):
            return ctx.enter_context(nc.sbuf_tensor(name, shape, dt))

        def sem(name):
            return ctx.enter_context(nc.semaphore(name))

        def bank(name):
            return ctx.enter_context(nc.psum_tensor(name, [P, 512], F32))

        ident = sb("ident", [P, P])
        ones = sb("ones", [P, P])
        zeros = sb("zeros", [P, 512], BF16)
        node_key = sb("node_key", [P, N])
        row_off = sb("row_off", [P, TILES])
        neg_half = sb("neg_half", [P, TILES])
        gate_in = sb("gate_in", [P, 1])
        gate_out = sb("gate_out", [P, 1 + TILES])
        dve_gate = sb("dve_gate", [P, 1 + 2 * HALVES + TILES])
        x_facts = sb("x_facts", [P, TILES, H + FACTS])
        adj_j = sb("adj_j", [P, TILES, N], I32)
        adj_i = sb("adj_i", [P, TILES, N], I32)
        x_t = sb("x_t", [P, N])
        w_ih = sb("w_ih", [P, 3 * H])
        w_hh = sb("w_hh", [P, 3 * H])
        b_ih = sb("b_ih", [P, 3])
        b_hh = sb("b_hh", [P, 3])
        w_att = sb("w_att", [P, H])
        w_ext = sb("w_ext", [P, H + 1])
        a_att = sb("a_att", [P, 2])
        t_dense = sb("t_dense", [P, A_BATCHES, BLOCK, TILES * H])
        x_dense = sb("x_dense", [P, 2, BLOCK, TILES, H])
        dense_sums = sb("dense_sums", [P, PER_TILE])
        dense_junk = sb("dense_junk", [P, BLOCK, P])
        key = sb("key", [P, HALVES, HALF])
        top = sb("top", [P, HALVES, 2 * TOP])
        idx = sb("idx", [P, HALVES, FIRST], U32)
        rows = sb("rows", [P, A_BATCHES, max(A_SIZES), H])
        hot = sb("hot", [P, HOTS, max(A_SIZES), SPARSE])
        adj_f = sb("adj_f", [P, TILES, N])
        scratch = sb("scratch", [P, TILES, N])
        count = sb("count", [P, TILES, HALVES])
        over = sb("over", [P, TILES, HALVES])
        leaves = sb("leaves", [P, TILES])
        order_key = sb("order_key", [P, TILES])
        neg_order = sb("neg_order", [P, TILES])
        diag = sb("diag", [P, TILES, P])
        rank_sum = sb("rank_sum", [P, TILES])
        rank_key = sb("rank_key", [P, TILES])
        perm = sb("perm", [P, TILES, N])
        s_facts = sb("s_facts", [P, TILES, FACTS])
        s_adj = sb("s_adj", [P, TILES, SPARSE])
        s_key = sb("s_key", [P, TILES, SPARSE])
        s_top = sb("s_top", [P, NB, TOP])
        s_row = sb("s_row", [P, NB, TOP], U32)
        left_f = sb("left_f", [P, TILES])
        left_sum = sb("left_sum", [P, 1])
        left = sb("left", [P, TILES + 1], I32)
        c_top = sb("c_top", [P, TOP])
        c_idx = sb("c_idx", [P, TOP], U32)
        b_rz = sb("b_rz", [P, 2])
        b_hn = sb("b_hn", [P, 1])
        agg = sb("agg", [P, N])
        hn_half = sb("hn_half", [P, N])
        th_r = sb("th_r", [P, N])
        th_z = sb("th_z", [P, N])
        n_in = sb("n_in", [P, N])
        n_gate = sb("n_gate", [P, N])
        x_part = sb("x_part", [P, N])
        one_z = sb("one_z", [P, N])
        n_part = sb("n_part", [P, N])
        stats = sb("stats", [P, TILES, 6])
        moments = sb("moments", [P, TILES, 2])
        var_eps = sb("var_eps", [P, TILES])
        rstd = sb("rstd", [P, TILES])
        shift = sb("shift", [P, 1])
        stats2 = sb("stats2", [P, TILES, 6])
        moments2 = sb("moments2", [P, TILES, 2])
        var_eps2 = sb("var_eps2", [P, TILES])
        rstd2 = sb("rstd2", [P, TILES])
        x1 = sb("x1", [P, TILES, H])
        x1_t = sb("x1_t", [P, N])
        att2 = sb("att2", [P, 1])
        att2_all = sb("att2_all", [P, P])
        bound = sb("bound", [P, TILES, N])
        e_ext = sb("e_ext", [P, TILES, H + 1])
        score, leaky, masked = adj_f, scratch, perm
        top_score = sb("top_score", [P, TILES])
        neg_top = sb("neg_top", [P, TILES])
        prob = sb("prob", [P, TILES, N])
        prob_sum = sb("prob_sum", [P, TILES])
        prob_t = sb("prob_t", [P, TILES, TILES, P])
        x1_scaled = sb("x1_scaled", [P, TILES, H])
        eps_scaled = sb("eps_scaled", [P, TILES])
        y2 = sb("y2", [P, TILES, H])
        out_sb = sb("out_sb", [P, TILES, H])

        ps_agg, ps_key, ps_x, ps_sx, ps_a, ps_b, ps_r, ps_z = (
            bank(f"ps_{n}") for n in ("agg", "key", "x", "sx", "a", "b", "r", "z"))
        SORTED_BANKS = (ps_sx, ps_b)
        DENSE_BANKS = (ps_a, ps_r)
        R_BANKS = (ps_r, ps_a)
        Z_BANKS = (ps_z, ps_x)
        N_BANKS = (ps_sx, ps_b)
        Y_PLACES = ((ps_agg, 0), (ps_agg, 1), (ps_r, 0), (ps_z, 0))
        X1_BANKS = (ps_key, ps_x)
        E_BANKS = (ps_b, ps_sx)
        ps_t = ps_z
        PROB_BANKS = (ps_key, ps_x, ps_r, ps_a)
        OUT_BANKS = (ps_agg, ps_b, ps_sx, ps_z)

        adj_in = [sem(f"adj_in{c}") for c in range(TILES)]
        x_in, adj_i_in, gru_in, att_in = (sem(n) for n in ("x_in", "adj_i_in", "gru_in", "att_in"))
        key_made, consts_ready, ident_zero, gate_set = (
            sem(n) for n in ("key_made", "consts_ready", "ident_zero", "gate_set"))
        key_in_psum, x_in_psum = sem("key_in_psum"), sem("x_in_psum")
        key_ready, top_ready, idx_ready, pool_gated = (
            sem(n) for n in ("key_ready", "top_ready", "idx_ready", "pool_gated"))
        gathered = [sem(f"gathered{b}") for b in range(A_BATCHES)]
        made = sem("made")
        hot_free = sem("hot_free")
        dense_in = [sem(f"dense_in{b}") for b in range(A_BATCHES)]
        x_dense_ready, dense_done, dense_copied = (sem(n) for n in ("x_dense_ready", "dense_done", "dense_copied"))
        dense_summed = sem("dense_summed")
        sized, counted, over_ready, leaves_ready, order_ready, neg_order_ready = (
            sem(n) for n in ("sized", "counted", "over_ready", "leaves_ready", "order_ready", "neg_order_ready"))
        diag_ready, order_spread, ranked, rank_key_ready, perm_ready = (
            sem(n) for n in ("diag_ready", "order_spread", "ranked", "rank_key_ready", "perm_ready"))
        adj_f_ready, facts_ready, x_sorted, adj_sorted = (
            sem(n) for n in ("adj_f_ready", "facts_ready", "x_sorted", "adj_sorted"))
        s_facts_ready, s_adj_ready, left_f_ready, left_ready = (
            sem(n) for n in ("s_facts_ready", "s_adj_ready", "left_f_ready", "left_ready"))
        all_keys_ready, s_key_ready, s_top_ready, s_row_ready = (
            sem(n) for n in ("all_keys_ready", "s_key_ready", "s_top_ready", "s_row_ready"))
        c_key_ready, c_top_ready, c_idx_ready, c_gathered, c_made, c_left, c_pool_gated, c_dve_gated = (
            [sem(f"{n}{t}") for t in range(TILES)]
            for n in ("c_key_ready", "c_top_ready", "c_idx_ready", "c_gathered", "c_made", "c_left",
                      "c_pool_gated", "c_dve_gated"))
        bias_sum, bias_ready, hn_done, hn_ready, agg_done, agg_copied, gates_done = (
            sem(n) for n in ("bias_sum", "bias_ready", "hn_done", "hn_ready", "agg_done", "agg_copied", "gates_done"))
        tanh_r, tanh_z, r_hn, n_sum, n_ready, x_part_ready, one_z_ready, n_part_ready = (
            sem(n) for n in ("tanh_r", "tanh_z", "r_hn", "n_sum", "n_ready", "x_part_ready", "one_z_ready",
                             "n_part_ready"))
        y_turned, stats_ready, moments_ready, var_ready, rstd_ready, shift_ready = (
            sem(n) for n in ("y_turned", "stats_ready", "moments_ready", "var_ready", "rstd_ready", "shift_ready"))
        x1_low, x1_high, x1_turned, x1_t_low, x1_t_high = (
            sem(n) for n in ("x1_low", "x1_high", "x1_turned", "x1_t_low", "x1_t_high"))
        att_done, att2_ready, w_ext_ready, att_all_ready, bound_ready = (
            sem(n) for n in ("att_done", "att2_ready", "w_ext_ready", "att_all_ready", "bound_ready"))
        e_done, e_low, e_high, target_done, score_ready, leaky_ready, top_score_ready, neg_top_ready = (
            sem(n) for n in ("e_done", "e_low", "e_high", "target_done", "score_ready", "leaky_ready",
                             "top_score_ready", "neg_top_ready"))
        prob_ready, prob_turned, prob_t_ready, mixed, scaled = (
            sem(n) for n in ("prob_ready", "prob_turned", "prob_t_ready", "mixed", "scaled"))
        y2_ready, stats2_ready, moments2_ready, var2_ready, rstd2_ready, out_ready, stored = (
            sem(n) for n in ("y2_ready", "stats2_ready", "moments2_ready", "var2_ready", "rstd2_ready",
                             "out_ready", "stored"))
        CONSTS = 5

        def sorted_x(t, n=H, to=0):
            return SORTED_BANKS[t // 2][:, (t % 2) * (H + FACTS) + to:(t % 2) * (H + FACTS) + to + n]

        def half_of(h):
            return slice(h * (N // 2), (h + 1) * (N // 2))

        def y_rows(t):
            bank, place = Y_PLACES[t]
            return bank[:, place * P:(place + 1) * P]

        block = ctx.enter_context(nc.Block())

        @block.sync
        def _(sp):
            adjT_v = adjT.rearrange("(p c) i -> p c i", c=TILES)
            for c in range(TILES):
                sp.dma_start(adj_j[:, c, :], adjT_v[:, c, :]).then_inc(adj_in[c], 16)
                if c == 0:
                    sp.dma_start(x_facts[:, :, 0:H], x.rearrange("(p c) h -> p c h", c=TILES)).then_inc(x_in, 16)
            for to, of in ((x_t, xT), (w_ih, w_ihT), (w_hh, w_hhT), (b_ih, b_ihT), (b_hh, b_hhT)):
                sp.dma_start(to[:, :], of).then_inc(gru_in, 16)
            for to, of in ((w_att[:, :], W), (w_ext[:, 0:H], WT), (a_att[:, :], aT)):
                sp.dma_start(to, of).then_inc(att_in, 16)
            sp.dma_start(adj_i[:, :, :], adj.rearrange("(c p) j -> p c j", p=P)).then_inc(adj_i_in, 16)
            T_v = T.rearrange("(i p c) h -> p i (c h)", p=P, c=TILES)
            for k in range(BLOCKS):
                if k >= A_BATCHES:
                    sp.wait_ge(dense_done, k - A_BATCHES + 1)
                i = SPARSE + k * BLOCK
                sp.dma_start(t_dense[:, k % A_BATCHES, :, :], T_v[:, i:i + BLOCK, :]).then_inc(
                    dense_in[k % A_BATCHES], 16)
            out_v = out.rearrange("(c p) h -> c p h", p=P)
            for t in range(TILES):
                sp.wait_ge(out_ready, t + 1)
                sp.dma_start(out_v[t], out_sb[:, t, :]).then_inc(stored, 16)
            sp.wait_ge(stored, 16 * TILES)

        @block.gpsimd
        def _(pool):
            pool.iota(node_key[:, :], [[N, N]], base=N, channel_multiplier=0,
                      allow_small_or_imprecise_dtypes=True).then_inc(key_made, 1)
            pool.iota(row_off[:, :], [[1, TILES]], base=-N, channel_multiplier=TILES,
                      allow_small_or_imprecise_dtypes=True).then_inc(key_made, 1)
            pool.memset(ident[:, :], 0.0).then_inc(ident_zero, 1)
            pool.memset(ones[:, :], 1.0).then_inc(consts_ready, 1)
            pool.memset(zeros[:, :], 0.0).then_inc(consts_ready, 1)
            pool.memset(neg_half[:, :], -0.5).then_inc(consts_ready, 1)
            pool.memset(gate_in[:, :], 0.0).then_inc(consts_ready, 1)
            pool.memset(gate_out[:, :], 0.0).then_inc(pool_gated, 1)
            pool.wait_ge(ident_zero, 1)
            pool.affine_select(out=ident[:, :], in_=ident[:, :], compare_op=ALU.not_equal, fill=1.0, base=0,
                               pattern=[[-1, P]], channel_multiplier=1).then_inc(consts_ready, 1)

            def gate(passed, before, place=0):
                pool.wait_ge(passed, before)
                return pool.tensor_tensor(gate_out[:, place:place + 1], gate_in[:, :], gate_in[:, :], ALU.mult)

            def gather(to, at):
                return pool.indirect_dma_start(to, None, T, bass.IndirectOffsetOnAxis(ap=at, axis=0))

            def gather_a(h, first, last):
                for m in range(first, last):
                    q = max(q for q in range(PER_HALF) if sum(A_SIZES[:q]) <= m)
                    b = h * PER_HALF + q
                    gather(rows[:, b, m - sum(A_SIZES[:q]), :], idx[:, h, m:m + 1]).then_inc(gathered[b], 16)

            for h in range(HALVES):
                pool.wait_ge(idx_ready, 2 * h + 1)
                gather_a(h, 0, TOP)
                pool.wait_ge(idx_ready, 2 * h + 2)
                gather_a(h, TOP, FIRST)
            pool.wait_ge(consts_ready, CONSTS)
            with pool.Fori(0, TILES - 1) as c:
                for h in range(HALVES):
                    pool.wait_ge(idx_ready, c * (2 * HALVES) + (2 * HALVES + 2 * h + 2))
                    pool.wait_ge(hot_free, c * A_BATCHES + (PER_HALF * (h + 1) + HOTS))
                    gate(pool_gated, c * HALVES + (h + 1)).then_inc(pool_gated, 1)
                    gather_a(h, 0, FIRST)
            for j, (r, first, n) in enumerate(B_BATCHES):
                g = A_ALL + j
                pool.wait_ge(s_row_ready, r + 1)
                pool.wait_ge(hot_free, HOTS + g - A_BATCHES + 1)
                for k in range(n):
                    gather(rows[:, g % A_BATCHES, k, :], s_row[:, r, first + k:first + k + 1]).then_inc(
                        gathered[g % A_BATCHES], 16)
            pool.wait_ge(left_ready, 2)
            all_left = pool.value_load(left[0:1, TILES:TILES + 1], min_val=0, max_val=TILES * N)
            with pool.If(all_left > 0):
                n_left = [pool.value_load(left[0:1, t:t + 1], min_val=0, max_val=N) for t in range(TILES)]
                for t in range(TILES):
                    with pool.If(n_left[t] > 0):
                        pool.memset(gate_out[:, 1 + t:2 + t], 0.0).then_inc(c_pool_gated[t], TOP)
                        with pool.Fori(0, n_left[t], TOP) as i:
                            pool.wait_ge(c_idx_ready[t], i + TOP)
                            gate(c_pool_gated[t], i + TOP, 1 + t).then_inc(c_pool_gated[t], TOP)
                            for k in range(TOP):
                                gather(rows[:, k // BATCH, k % BATCH, :], c_idx[:, k:k + 1]).then_inc(c_gathered[t], 16)
            for h in range(HALVES):
                half = half_of(h)
                pool.wait_ge(tanh_z, h + 1)
                pool.tensor_scalar(one_z[:, half], th_z[:, half], -1.0, 1.0, ALU.mult, ALU.add).then_inc(one_z_ready, 1)
            for u in range(2):
                pair = slice(2 * u, 2 * u + 2)
                pool.wait_ge(var_ready, u + 1)
                pool.tensor_tensor(rstd[:, pair], var_eps[:, pair], neg_half[:, pair], ALU.pow).then_inc(rstd_ready, 1)
            for t in range(TILES):
                pool.wait_ge(prob_ready, t + 1)
                pool.wait_ge(x1_low, 2)
                pool.wait_ge(x1_high, 2)
                pool.tensor_scalar(x1_scaled[:, t, :], x1[:, t, :], prob_sum[:, t:t + 1], None, ALU.mult).then_inc(
                    scaled, 1)
                pool.tensor_scalar(eps_scaled[:, t:t + 1], prob_sum[:, t:t + 1], prob_sum[:, t:t + 1], EPS,
                                   ALU.mult, ALU.mult).then_inc(scaled, 1)
            for t in range(TILES):
                pool.wait_ge(var2_ready, t + 1)
                pool.tensor_tensor(rstd2[:, t:t + 1], var_eps2[:, t:t + 1], neg_half[:, 0:1], ALU.pow).then_inc(
                    rstd2_ready, 1)

        @block.vector
        def _(dve):
            def gate(place):
                return dve.tensor_copy(dve_gate[:, 1 + place:2 + place], dve_gate[:, 0:1])

            def times_key(to, adjacency, keys):
                return dve.scalar_tensor_tensor(out=to, in0=adjacency, scalar=0.0, in1=keys,
                                                op0=ALU.not_equal, op1=ALU.mult)

            def row_index(to, of, offset):
                return dve.tensor_scalar(to, of, offset, 0.0, ALU.add, ALU.max)

            def find_a(c, h):
                half = slice(h * HALF, (h + 1) * HALF)
                done = c * (2 * HALVES) + 2 * h
                off = row_off[:, bass.ds(c, 1)]
                times_key(key[:, h, :], adj_j[:, c, half], node_key[:, half]).then_inc(key_ready, 1)
                dve.wait_ge(key_ready, done + 1)
                gate(2 * h)
                dve.max(top[:, h, 0:TOP], key[:, h, :]).then_inc(top_ready, 1)
                dve.wait_ge(top_ready, done + 1)
                row_index(idx[:, h, 0:TOP], top[:, h, 0:TOP], off).then_inc(idx_ready, 1)
                dve.match_replace(key[:, h, :], top[:, h, 0:TOP], key[:, h, :], 0.0).then_inc(key_ready, 1)
                dve.wait_ge(key_ready, done + 2)
                gate(2 * h + 1)
                dve.max(top[:, h, TOP:2 * TOP], key[:, h, :]).then_inc(top_ready, 1)
                dve.wait_ge(top_ready, done + 2)
                row_index(idx[:, h, TOP:FIRST], top[:, h, TOP:FIRST], off).then_inc(idx_ready, 1)
                dve.tensor_copy(x_facts[:, bass.ds(c, 1), H + 2 + h:H + 3 + h].rearrange("p c f -> p (c f)"),
                                top[:, h, FIRST - 1:FIRST]).then_inc(facts_ready, 1)

            def sum_dense(k, b, to):
                dve.wait_ge(dense_done, k + 1)
                dve.wait_ge(dense_summed, k + 2)
                for r in range(BLOCK):
                    last = dve.tensor_tensor_reduce(out=dense_junk[:, r, :],
                                                    in0=DENSE_BANKS[b % 2][:, r * P:(r + 1) * P], in1=ident[:, :],
                                                    scale=1.0, scalar=0.0, op0=ALU.mult, op1=ALU.add,
                                                    accum_out=to(r))
                last.then_inc(dense_summed, 1)

            def times_x(batch, n, features):
                return dve.tensor_tensor(rows[:, batch, 0:n, :], rows[:, batch, 0:n, :],
                                         features.unsqueeze(1).to_broadcast([P, n, H]), ALU.mult)

            def edges_a(c, b, between=()):
                assert len(between) <= A_SIZES[b % PER_HALF]
                h, q = b // PER_HALF, b % PER_HALF
                half = slice(h * HALF, (h + 1) * HALF)
                dve.wait_ge(hot_free, c * A_BATCHES + (b + 1))
                for k in range(A_SIZES[q]):
                    m = sum(A_SIZES[:q]) + k
                    dve.scalar_tensor_tensor(out=hot[:, b % HOTS, k, 0:HALF], in0=ps_key[:, half],
                                             scalar=top[:, h, m:m + 1], in1=adj_j[:, c, half],
                                             op0=ALU.is_equal, op1=ALU.mult)
                    if k < len(between):
                        between[k]()
                dve.wait_ge(gathered[b], c * (16 * A_SIZES[q]) + 16 * A_SIZES[q])
                times_x(b, A_SIZES[q], ps_x[:, bass.ds(c * H, H)]).then_inc(made, 1)

            dve.memset(dve_gate[:, :], 0.0).then_inc(gate_set, 1)
            dve.memset(dense_sums[:, :], 0.0).then_inc(dense_summed, 2)
            dve.wait_ge(gate_set, 1)
            dve.wait_ge(key_made, 2)
            dve.wait_ge(adj_in[0], 16)
            find_a(0, 0)
            find_a(0, 1)
            dve.wait_ge(counted, TILES * HALVES)
            dve.tensor_scalar(over[:, :, :], count[:, :, :], -float(FIRST), 0.0, ALU.add, ALU.max).then_inc(
                over_ready, 1)
            dve.wait_ge(over_ready, 1)
            dve.tensor_tensor(leaves[:, :], over[:, :, 0], over[:, :, 1], ALU.add).then_inc(leaves_ready, 1)
            dve.wait_ge(leaves_ready, 1)
            dve.scalar_tensor_tensor(out=order_key[:, :], in0=leaves[:, :], scalar=float(N), in1=row_off[:, :],
                                     op0=ALU.mult, op1=ALU.add).then_inc(order_ready, 1)
            dve.tensor_copy(x_facts[:, :, H], row_off[:, :]).then_inc(facts_ready, 1)
            dve.tensor_copy(x_facts[:, :, H + 1], leaves[:, :]).then_inc(facts_ready, 1)
            dve.wait_ge(order_ready, 1)
            dve.tensor_scalar(neg_order[:, :], order_key[:, :], -1.0, None, ALU.mult).then_inc(neg_order_ready, 1)

            dve.wait_ge(key_in_psum, 1)
            dve.wait_ge(ranked, TILES)
            dve.tensor_scalar(rank_key[:, :], rank_sum[:, :], N / 2.0, N * (N - 1) / 2.0 + N, ALU.mult,
                              ALU.add).then_inc(rank_key_ready, 1)
            dve.wait_ge(rank_key_ready, 1)
            for c in range(TILES):
                dve.tensor_scalar(perm[:, c, :], ps_key[:, :], rank_key[:, c:c + 1], None,
                                  ALU.is_equal).then_inc(perm_ready, 1)
            def keys_b(c):
                dve.wait_ge(s_adj_ready, c + 1)
                times_key(s_key[:, bass.ds(c, 1), :].rearrange("p c i -> p (c i)"),
                          s_adj[:, bass.ds(c, 1), :].rearrange("p c i -> p (c i)"), node_key[:, 0:SPARSE]).then_inc(
                    all_keys_ready, 1)

            for h in range(HALVES):
                for b in range(h * PER_HALF, (h + 1) * PER_HALF):
                    edges_a(0, b)
                find_a(1, h)
            keys_b(0)
            with dve.Fori(FIRST_TILE, TILES - 1) as c:
                def sum_dense_tile(b):
                    sum_dense((c - FIRST_TILE) * A_BATCHES + b, b,
                              lambda r: dense_sums[:, b * BLOCK + r:b * BLOCK + r + 1])

                for h in range(HALVES):
                    for b in range(h * PER_HALF, (h + 1) * PER_HALF):
                        edges_a(c, b)
                        if b >= 1:
                            sum_dense_tile(b - 1)
                    find_a(c + 1, h)
                keys_b(c)
                sum_dense_tile(A_BATCHES - 1)
                dve.wait_ge(dense_summed, (c - FIRST_TILE) * A_BATCHES + (A_BATCHES + 2))
                dve.tensor_copy(agg[:, bass.ds((c - FIRST_TILE) * PER_TILE + SPARSE, PER_TILE)],
                                dense_sums[:, :]).then_inc(dense_copied, 1)
                dve.wait_ge(dense_copied, c)

            def sum_dense_static(k):
                sum_dense(k, k % A_BATCHES, lambda r: agg[:, SPARSE + k * BLOCK + r:SPARSE + k * BLOCK + r + 1])

            def find_b(r):
                t, n = B_ROUNDS[r]
                base = S_KEYS[t]

                def narrow():
                    dve.wait_ge(all_keys_ready, t + 1)
                    for h in range(HALVES):
                        half = slice(h * HALF, (h + 1) * HALF)
                        dve.scalar_tensor_tensor(out=s_key[:, t, half], in0=node_key[:, half],
                                                 scalar=s_facts[:, t, 2 + h:3 + h], in1=s_key[:, t, half],
                                                 op0=ALU.is_lt, op1=ALU.mult).then_inc(s_key_ready, 1)

                def largest():
                    dve.wait_ge(s_key_ready, base + 2 + (r - B_FIRST[t]))
                    dve.max(s_top[:, r, :], s_key[:, t, :]).then_inc(s_top_ready, 1)

                def index():
                    dve.wait_ge(s_top_ready, r + 1)
                    row_index(s_row[:, r, :], s_top[:, r, :], s_facts[:, t, 0:1]).then_inc(s_row_ready, 1)
                    if r != B_LAST[t]:
                        dve.match_replace(s_key[:, t, :], s_top[:, r, :], s_key[:, t, :], 0.0).then_inc(s_key_ready, 1)

                return ([narrow] if r == B_FIRST[t] else []) + [largest, index]

            def edges_b(r, between=()):
                t, _ = B_ROUNDS[r]
                for j, (of, first, n) in enumerate(B_BATCHES):
                    if of != r:
                        continue
                    g = A_ALL + j
                    assert first > 0 or len(between) <= n
                    dve.wait_ge(hot_free, g + 1)
                    for k in range(n):
                        dve.scalar_tensor_tensor(out=hot[:, g % HOTS, k, :], in0=ps_key[:, 0:SPARSE],
                                                 scalar=s_top[:, r, first + k:first + k + 1], in1=s_adj[:, t, :],
                                                 op0=ALU.is_equal, op1=ALU.mult)
                        if first == 0 and k < len(between):
                            between[k]()
                    dve.wait_ge(gathered[g % A_BATCHES], arrived(g))
                    times_x(g % A_BATCHES, n, sorted_x(t)).then_inc(made, 1)
                    if j <= B_DENSE:
                        sum_dense_static(BLOCKS - B_DENSE + j - 1)

            dve.wait_ge(s_adj_ready, TILES)
            times_key(s_key[:, TILES - 1, :], s_adj[:, TILES - 1, :], node_key[:, 0:SPARSE]).then_inc(
                all_keys_ready, 1)
            for b in range(A_BATCHES):
                edges_a(TILES - 1, b, find_b(b - 1) if 1 <= b <= B_AHEAD else ())
                if b >= 1:
                    sum_dense_static(BLOCKS - B_DENSE - A_BATCHES + b - 1)
                if b == 0:
                    dve.wait_ge(x_sorted, 1)
                    for u in range(2):
                        dve.tensor_copy(s_facts[:, 2 * u:2 * u + 2, :],
                                        SORTED_BANKS[u][:, 0:2 * (H + FACTS)].rearrange(
                                            "p (t f) -> p t f", t=2)[:, :, H:H + FACTS]).then_inc(s_facts_ready, 1)
                    dve.wait_ge(s_facts_ready, 2)
                    for t in range(TILES):
                        dve.tensor_scalar(left_f[:, t:t + 1], s_facts[:, t, 1:2], -float(CAPS[t]), 0.0, ALU.add,
                                          ALU.max).then_inc(left_f_ready, 1)
                    dve.wait_ge(left_f_ready, TILES)
                    dve.tensor_copy(left[:, 0:TILES], left_f[:, :]).then_inc(left_ready, 1)
                    dve.reduce_sum(left_sum[:, :], left_f[:, :], axis=mybir.AxisListType.X).then_inc(
                        left_f_ready, 1)
                    dve.wait_ge(left_f_ready, TILES + 1)
                    dve.tensor_copy(left[:, TILES:TILES + 1], left_sum[:, :]).then_inc(left_ready, 1)
            for r in range(NB):
                edges_b(r, find_b(r + B_AHEAD) if r + B_AHEAD < NB else ())

            dve.wait_ge(left_ready, 2)
            all_left = dve.value_load(left[0:1, TILES:TILES + 1], min_val=0, max_val=TILES * N)
            with dve.If(all_left > 0):
                n_left = [dve.value_load(left[0:1, t:t + 1], min_val=0, max_val=N) for t in range(TILES)]
                for t in range(TILES):
                    with dve.If(n_left[t] > 0):
                        dve.memset(dve_gate[:, 1 + 2 * HALVES + t:2 + 2 * HALVES + t], 0.0).then_inc(c_dve_gated[t], TOP)
                        for h in range(HALVES):
                            half = slice(h * HALF, (h + 1) * HALF)
                            dve.scalar_tensor_tensor(out=s_key[:, t, half], in0=node_key[:, half],
                                                     scalar=s_facts[:, t, 2 + h:3 + h], in1=s_adj[:, t, half],
                                                     op0=ALU.is_lt, op1=ALU.mult).then_inc(c_key_ready[t], 1)
                        final = B_ROUNDS[B_LAST[t]][1] - 1
                        dve.wait_ge(c_key_ready[t], 2)
                        dve.scalar_tensor_tensor(out=s_key[:, t, :], in0=node_key[:, 0:SPARSE],
                                                 scalar=s_top[:, B_LAST[t], final:final + 1], in1=s_key[:, t, :],
                                                 op0=ALU.is_lt, op1=ALU.mult).then_inc(c_key_ready[t], 1)
                        dve.wait_ge(c_key_ready[t], 3)
                        times_key(s_key[:, t, :], s_key[:, t, :], node_key[:, 0:SPARSE]).then_inc(
                            c_key_ready[t], TOP - 3)
                        dve.wait_ge(hot_free, ALL + HOTS)
                        with dve.Fori(0, n_left[t], TOP) as i:
                            dve.wait_ge(c_key_ready[t], i + TOP)
                            dve.wait_ge(c_dve_gated[t], i + TOP)
                            gate(2 * HALVES + t).then_inc(c_dve_gated[t], TOP)
                            dve.max(c_top[:, :], s_key[:, t, :]).then_inc(c_top_ready[t], TOP)
                            dve.wait_ge(c_top_ready[t], i + TOP)
                            row_index(c_idx[:, :], c_top[:, :], s_facts[:, t, 0:1]).then_inc(c_idx_ready[t], TOP)
                            dve.match_replace(s_key[:, t, :], c_top[:, :], s_key[:, t, :], 0.0).then_inc(
                                c_key_ready[t], TOP)
                            for k in range(TOP):
                                dve.scalar_tensor_tensor(out=hot[:, k // BATCH, k % BATCH, :], in0=ps_key[:, 0:SPARSE],
                                                         scalar=c_top[:, k:k + 1], in1=s_adj[:, t, :],
                                                         op0=ALU.is_equal, op1=ALU.mult)
                            dve.wait_ge(c_gathered[t], i * 16 + 16 * TOP)
                            for b in range(TOP // BATCH):
                                times_x(b, BATCH, sorted_x(t)).then_inc(c_made[t], BATCH)
                            dve.wait_ge(c_left[t], i + TOP)

            def n_input(h):
                half = half_of(h)
                dve.wait_ge(tanh_r, h + 1)
                dve.wait_ge(hn_ready, 1)
                dve.scalar_tensor_tensor(out=n_in[:, half], in0=th_r[:, half], scalar=1.0, in1=hn_half[:, half],
                                         op0=ALU.add, op1=ALU.mult).then_inc(r_hn, 1)
                dve.wait_ge(r_hn, h + 1)
                dve.wait_ge(gates_done, 3 * h + 2)
                dve.tensor_tensor(n_in[:, half], n_in[:, half], N_BANKS[h][:, 0:N // 2], ALU.add).then_inc(n_sum, 1)

            def x_weighted(h):
                half = half_of(h)
                dve.wait_ge(tanh_z, h + 1)
                dve.scalar_tensor_tensor(out=x_part[:, half], in0=th_z[:, half], scalar=3.0, in1=x_t[:, half],
                                         op0=ALU.add, op1=ALU.mult).then_inc(x_part_ready, 1)

            def n_weighted(h):
                half = half_of(h)
                dve.wait_ge(one_z_ready, h + 1)
                dve.wait_ge(n_ready, h + 1)
                dve.tensor_tensor(n_part[:, half], n_gate[:, half], one_z[:, half], ALU.mult).then_inc(
                    n_part_ready, 1)

            n_input(0)
            x_weighted(0)
            n_input(1)
            n_weighted(0)
            x_weighted(1)
            n_weighted(1)

            for u in range(2):
                dve.wait_ge(y_turned, u + 1)
                for t in (2 * u, 2 * u + 1):
                    dve.bn_stats(stats[:, t, :], y_rows(t)).then_inc(stats_ready, 1)
                for t in (2 * u, 2 * u + 1):
                    dve.wait_ge(stats_ready, t + 1)
                    dve.bn_aggr(moments[:, t, :], stats[:, t, :]).then_inc(moments_ready, 1)
                dve.wait_ge(moments_ready, 2 * u + 2)
                dve.tensor_scalar(var_eps[:, 2 * u:2 * u + 2], moments[:, 2 * u:2 * u + 2, 1], 4 * EPS, None,
                                  ALU.add).then_inc(var_ready, 1)
            dve.wait_ge(rstd_ready, 1)
            for t in range(2):
                dve.tensor_scalar(x1[:, t, :], y_rows(t), moments[:, t, 0:1], rstd[:, t:t + 1],
                                  ALU.subtract, ALU.mult).then_inc(x1_low, 1)
            dve.wait_ge(rstd_ready, 2)
            dve.scalar_tensor_tensor(out=shift[:, :], in0=moments[:, 3:4, 0], scalar=-1.0, in1=rstd[:, 3:4],
                                     op0=ALU.mult, op1=ALU.mult).then_inc(shift_ready, 1)
            dve.tensor_scalar(x1[:, 2, :], y_rows(2), moments[:, 2, 0:1], rstd[:, 2:3],
                              ALU.subtract, ALU.mult).then_inc(x1_high, 1)
            dve.wait_ge(x1_turned, 1)
            dve.tensor_copy(x1_t[:, 0:2 * P], X1_BANKS[0][:, 0:2 * P]).then_inc(x1_t_low, 1)
            for u, ready in enumerate((e_low, e_high)):
                dve.wait_ge(e_done, u + 1)
                dve.tensor_copy(e_ext[:, 2 * u:2 * u + 2, :].rearrange("p t h -> p (t h)"),
                                E_BANKS[u][:, 0:2 * (H + 1)]).then_inc(ready, 1)

            def leaky_relu(t):
                dve.wait_ge(score_ready, t + 1)
                dve.scalar_tensor_tensor(out=leaky[:, t, :], in0=score[:, t, :], scalar=0.01, in1=score[:, t, :],
                                         op0=ALU.mult, op1=ALU.max).then_inc(leaky_ready, 1)

            def mask(t):
                dve.wait_ge(leaky_ready, t + 1)
                dve.wait_ge(bound_ready, 3 * TILES)
                dve.tensor_tensor_reduce(out=masked[:, t, :], in0=leaky[:, t, :], in1=bound[:, t, :], scale=1.0,
                                         scalar=LEAST, op0=ALU.add, op1=ALU.max,
                                         accum_out=top_score[:, t:t + 1]).then_inc(top_score_ready, 1)

            def negate_top(t):
                dve.wait_ge(top_score_ready, t + 1)
                dve.tensor_scalar(neg_top[:, t:t + 1], top_score[:, t:t + 1], -1.0, None,
                                  ALU.mult).then_inc(neg_top_ready, 1)

            leaky_relu(0)
            mask(0)
            negate_top(0)
            leaky_relu(1)
            leaky_relu(2)
            mask(1)
            negate_top(1)
            leaky_relu(3)
            mask(2)
            negate_top(2)
            mask(3)
            negate_top(3)

            def normalise(t):
                dve.wait_ge(rstd2_ready, t + 1)
                dve.tensor_scalar(out_sb[:, t, :], y2[:, t, :], moments2[:, t, 0:1], rstd2[:, t:t + 1],
                                  ALU.subtract, ALU.mult).then_inc(out_ready, 1)

            for t in range(TILES):
                dve.wait_ge(mixed, t + 1)
                dve.wait_ge(scaled, 2 * t + 2)
                dve.scalar_tensor_tensor(out=y2[:, t, :], in0=OUT_BANKS[t][:, 0:H], scalar=0.0,
                                         in1=x1_scaled[:, t, :], op0=ALU.max, op1=ALU.add).then_inc(y2_ready, 1)
                if t >= 2:
                    normalise(t - 2)
                dve.wait_ge(y2_ready, t + 1)
                dve.bn_stats(stats2[:, t, :], y2[:, t, :]).then_inc(stats2_ready, 1)
                dve.wait_ge(stats2_ready, t + 1)
                dve.bn_aggr(moments2[:, t, :], stats2[:, t, :]).then_inc(moments2_ready, 1)
                dve.wait_ge(moments2_ready, t + 1)
                dve.tensor_tensor(var_eps2[:, t:t + 1], moments2[:, t, 1:2], eps_scaled[:, t:t + 1],
                                  ALU.add).then_inc(var2_ready, 1)
            normalise(2)
            normalise(3)

        @block.scalar
        def _(act):
            act.wait_ge(key_made, 1)
            act.copy(ps_key[:, :], node_key[:, :]).then_inc(key_in_psum, 1)
            for c in range(TILES):
                act.wait_ge(adj_in[c], 16)
                act.activation(scratch[:, c, :], adj_j[:, c, :], ACT.Abs).then_inc(sized, 1)
                act.wait_ge(sized, c + 1)
                for h in range(HALVES):
                    act.activation(adj_f[:, c, h * HALF:(h + 1) * HALF], scratch[:, c, h * HALF:(h + 1) * HALF],
                                   ACT.Sign, accum_out=count[:, c, h:h + 1]).then_inc(counted, 1)
                if c == 0:
                    act.wait_ge(x_in, 16)
                    act.copy(ps_x[:, :].rearrange("p (c h) -> p c h", h=H), x_facts[:, :, 0:H]).then_inc(x_in_psum, 1)
            act.wait_ge(consts_ready, CONSTS)
            act.wait_ge(order_ready, 1)
            for c in range(TILES):
                act.mul(diag[:, c, :], ident[:, :], order_key[:, c:c + 1]).then_inc(diag_ready, 1)
            act.wait_ge(neg_order_ready, 1)
            act.wait_ge(order_spread, 1)
            act.wait_ge(counted, TILES * HALVES)
            for c in range(TILES):
                act.activation(scratch[:, c, :], ps_a[:, :], ACT.Sign, bias=neg_order[:, c:c + 1],
                               accum_out=rank_sum[:, c:c + 1]).then_inc(ranked, 1)
            for c in range(TILES):
                act.copy(adj_f[:, c, :], adj_j[:, c, :]).then_inc(adj_f_ready, 1)
            act.wait_ge(gru_in, 16 * 5)
            for g in range(2):
                act.activation(b_rz[:, g:g + 1], b_ih[:, g:g + 1], ACT.Identity,
                               bias=b_hh[:, g:g + 1]).then_inc(bias_sum, 1)
            act.wait_ge(bias_sum, 2)
            act.mul(b_rz[:, :], b_rz[:, :], 0.5).then_inc(bias_ready, 1)
            act.mul(b_hn[:, :], b_hh[:, 2:3], 0.5).then_inc(bias_ready, 1)
            act.wait_ge(hn_done, 1)
            act.wait_ge(bias_ready, 2)
            act.activation(hn_half[:, :], ps_z[:, :], ACT.Identity, bias=b_hn[:, 0:1], scale=0.5).then_inc(hn_ready, 1)
            act.wait_ge(att_in, 16 * 3)
            act.wait_ge(att_done, 1)
            act.copy(w_ext[:, H:H + 1], ps_b[:, 0:1]).then_inc(w_ext_ready, 1)
            act.copy(att2[:, :], ps_b[:, 1:2]).then_inc(att2_ready, 1)
            act.wait_ge(att2_ready, 1)
            act.mul(att2_all[:, :], ones[:, :], att2[:, 0:1]).then_inc(att_all_ready, 1)
            def scale_x(k, u, column):
                for r in range(BLOCK):
                    for c in range(TILES):
                        last = act.activation(x_dense[:, u, r, c, :], x_facts[:, c, 0:H], ACT.Copy,
                                              scale=column(c, u * BLOCK + r))
                last.then_inc(x_dense_ready, 1)

            for k in range(2):
                scale_x(k, k, lambda c, r: adj_f[:, c, SPARSE + r:SPARSE + r + 1])
            for t in range(TILES):
                act.wait_ge(adj_sorted, t + 1)
                act.copy(s_adj[:, t, :], (ps_a, ps_r)[t % 2][:, 0:SPARSE]).then_inc(s_adj_ready, 1)
            with act.Fori(1, BLOCKS // 2) as g:
                for u in range(2):
                    act.wait_ge(dense_done, g * 2 + (u - 1))
                    scale_x(None, u, lambda c, r: adj_f[:, c, bass.ds(g * (2 * BLOCK) + (SPARSE + r), 1)])
            act.wait_ge(adj_i_in, 16)
            for t in range(TILES):
                act.activation(bound[:, t, :], adj_i[:, t, :], ACT.Relu).then_inc(bound_ready, 1)
                act.wait_ge(bound_ready, 3 * t + 1)
                act.activation(bound[:, t, :], bound[:, t, :], ACT.Sign).then_inc(bound_ready, 1)
                act.wait_ge(bound_ready, 3 * t + 2)
                act.activation(bound[:, t, :], bound[:, t, :], ACT.Copy, scale=-MASKED,
                               bias=MASKED).then_inc(bound_ready, 1)
            act.wait_ge(agg_done, 1)
            for part in (slice(0, N // 2), slice(N // 2, SPARSE)):
                act.copy(agg[:, part], ps_agg[:, part]).then_inc(agg_copied, 1)

            def gate_r(h):
                act.wait_ge(gates_done, 3 * h + 1)
                act.activation(th_r[:, half_of(h)], R_BANKS[h][:, 0:N // 2], ACT.Tanh, bias=b_rz[:, 0:1],
                               scale=0.5).then_inc(tanh_r, 1)

            def gate_z(h):
                act.wait_ge(gates_done, 3 * h + 3)
                act.activation(th_z[:, half_of(h)], Z_BANKS[h][:, 0:N // 2], ACT.Tanh, bias=b_rz[:, 1:2],
                               scale=0.5).then_inc(tanh_z, 1)

            def gate_n(h):
                act.wait_ge(n_sum, h + 1)
                act.activation(n_gate[:, half_of(h)], n_in[:, half_of(h)], ACT.Tanh, bias=b_ih[:, 2:3]).then_inc(
                    n_ready, 1)

            gate_r(0)
            gate_z(0)
            gate_r(1)
            gate_n(0)
            gate_z(1)
            gate_n(1)
            act.wait_ge(shift_ready, 1)
            act.activation(x1[:, 3, :], y_rows(3), ACT.Identity, bias=shift[:, :], scale=rstd[:, 3:4]).then_inc(
                x1_high, 1)
            act.wait_ge(x1_turned, 2)
            act.copy(x1_t[:, 2 * P:4 * P], X1_BANKS[1][:, 0:2 * P]).then_inc(x1_t_high, 1)
            act.wait_ge(target_done, 2)
            for t in range(TILES):
                act.wait_ge((e_low, e_high)[t // 2], 1)
                act.activation(score[:, t, :], ps_t[:, :], ACT.Identity, bias=e_ext[:, t, H:H + 1]).then_inc(
                    score_ready, 1)
            def copy_prob(t):
                act.wait_ge(prob_turned, t + 1)
                act.copy(prob_t[:, t, :, :].rearrange("p c i -> p (c i)"),
                         PROB_BANKS[t][:, :]).then_inc(prob_t_ready, 1)

            for t in range(TILES):
                act.wait_ge(neg_top_ready, t + 1)
                act.activation(prob[:, t, :], masked[:, t, :], ACT.Exp, bias=neg_top[:, t:t + 1],
                               accum_out=prob_sum[:, t:t + 1]).then_inc(prob_ready, 1)
                if t in (0, 2):
                    copy_prob(t // 2)
            copy_prob(2)
            copy_prob(3)

        @block.tensor
        def _(pe):
            pe.wait_ge(consts_ready, CONSTS)
            pe.matmul(ps_agg[:, :], zeros[:, 0:P], zeros[:, :], start=True, stop=False,
                      skip_group_check=True).then_inc(hot_free, HOTS)
            pe.wait_ge(gru_in, 16 * 5)
            pe.matmul(ps_z[:, :], w_hh[:, 2 * H:3 * H], x_t[:, :], start=True, stop=True).then_inc(hn_done, 1)
            pe.wait_ge(att_in, 16 * 3)
            pe.matmul(ps_b[:, 0:2], w_att[:, :], a_att[:, :], start=True, stop=True).then_inc(att_done, 1)
            for c in range(TILES):
                pe.wait_ge(diag_ready, c + 1)
                spread = pe.matmul(ps_a[:, c * P:(c + 1) * P], ones[:, :], diag[:, c, :], start=True, stop=True)
            spread.then_inc(order_spread, 1)

            def add_batch_a(b, ready):
                h = b // PER_HALF
                pe.wait_ge(made, ready)
                for k in range(A_SIZES[b % PER_HALF]):
                    last = pe.matmul(ps_agg[:, h * HALF:(h + 1) * HALF], rows[:, b, k, :],
                                     hot[:, b % HOTS, k, 0:HALF], start=False, stop=False, skip_group_check=True)
                last.then_inc(hot_free, 1)

            def sort_adj(t, part):
                if part == 0 and t >= 2:
                    pe.wait_ge(s_adj_ready, t - 1)
                for c in range(part * TILES // 2, (part + 1) * TILES // 2):
                    last = pe.matmul((ps_a, ps_r)[t % 2][:, 0:SPARSE], perm[:, c, t * P:(t + 1) * P],
                                     adj_f[:, c, 0:SPARSE],
                                     start=(c == 0), stop=(c == TILES - 1), skip_group_check=True)
                if part == 1:
                    last.then_inc(adj_sorted, 1)

            def add_dense(k, b, arrived_dense):
                pe.wait_ge(dense_in[b], arrived_dense)
                pe.wait_ge(x_dense_ready, k + 1)
                pe.wait_ge(dense_summed, k + 1)
                for r in range(BLOCK):
                    for c in range(TILES):
                        last = pe.matmul(DENSE_BANKS[b % 2][:, r * P:(r + 1) * P],
                                         t_dense[:, b, r, c * H:(c + 1) * H], x_dense[:, b % 2, r, c, :],
                                         start=(c == 0), stop=(c == TILES - 1))
                last.then_inc(dense_done, 1)

            def add_dense_static(k):
                add_dense(k, k % A_BATCHES, 16 * (k // A_BATCHES + 1))

            pe.wait_ge(perm_ready, TILES)
            pe.wait_ge(ranked, TILES)
            pe.wait_ge(adj_f_ready, TILES)
            parts = [(t, part) for t in range(TILES) for part in range(2)]
            for b in range(A_BATCHES):
                add_batch_a(b, b + 1)
                for t, part in parts[max(b, 2 * b - PER_HALF):max(b + 1, 2 * b - PER_HALF + 2)]:
                    sort_adj(t, part)
            pe.wait_ge(s_adj_ready, TILES)
            with pe.Fori(FIRST_TILE, TILES - 1) as c:
                for b in range(A_BATCHES):
                    add_dense((c - FIRST_TILE) * A_BATCHES + b, b, (c - FIRST_TILE) * 16 + 16)
                    add_batch_a(b, c * A_BATCHES + (b + 1))
            pe.wait_ge(facts_ready, 2 + TILES * HALVES)
            pe.wait_ge(x_in, 16)
            pe.wait_ge(att_all_ready, 1)
            for t in range(TILES):
                for c in range(TILES):
                    last = pe.matmul(sorted_x(t, H + FACTS), perm[:, c, t * P:(t + 1) * P], x_facts[:, c, :],
                                     start=(c == 0), stop=(c == TILES - 1))
            last.then_inc(x_sorted, 1)
            def open_gate(gate, h):
                pe.matmul((R_BANKS, Z_BANKS)[gate][h][:, 0:N // 2], w_hh[:, gate * H:(gate + 1) * H],
                          x_t[:, half_of(h)], start=True, stop=False, skip_group_check=True)

            for b in range(A_BATCHES):
                add_dense_static((TILES - 1 - FIRST_TILE) * A_BATCHES + b)
                if b == PER_HALF:
                    pe.wait_ge(hn_ready, 1)
                    open_gate(1, 0)
                add_batch_a(b, (TILES - 1) * A_BATCHES + b + 1)
            open_gate(1, 1)
            pe.wait_ge(left_ready, 2)
            all_left = pe.value_load(left[0:1, TILES:TILES + 1], min_val=0, max_val=TILES * N)
            for j, (r, first, n) in enumerate(B_BATCHES):
                g = A_ALL + j
                if j < B_DENSE:
                    add_dense_static(BLOCKS - B_DENSE + j)
                if j in (B_DENSE + 2, B_DENSE + 4):
                    pe.wait_ge(dense_summed, BLOCKS + 2)
                    open_gate(0, (j - B_DENSE) // 2 - 1)
                pe.wait_ge(made, g + 1)
                for k in range(n):
                    last = pe.matmul(ps_agg[:, 0:SPARSE], rows[:, g % A_BATCHES, k, :], hot[:, g % HOTS, k, :],
                                     start=False, stop=False, skip_group_check=True)
                last.then_inc(hot_free, 1)
            with pe.If(all_left > 0):
                n_left = [pe.value_load(left[0:1, t:t + 1], min_val=0, max_val=N) for t in range(TILES)]
                for t in range(TILES):
                    with pe.If(n_left[t] > 0):
                        with pe.Fori(0, n_left[t], TOP) as i:
                            for b in range(TOP // BATCH):
                                pe.wait_ge(c_made[t], i + (b + 1) * BATCH)
                                for k in range(BATCH):
                                    pe.matmul(ps_agg[:, 0:SPARSE], rows[:, b, k, :], hot[:, b, k, :], start=False, stop=False,
                                              skip_group_check=True).then_inc(c_left[t], 1)
            pe.matmul(ps_agg[:, :], zeros[:, 0:P], zeros[:, :], start=False, stop=True,
                      skip_group_check=True).then_inc(agg_done, 1)

            def stay_warm(n):
                for _ in range(n):
                    pe.matmul(ps_a[:, :], zeros[:, 0:P], zeros[:, :], start=True, stop=True)

            pe.wait_ge(dense_summed, BLOCKS + 2)
            pe.wait_ge(dense_copied, TILES - 1 - FIRST_TILE)
            for h in range(HALVES):
                pe.wait_ge(agg_copied, h + 1)
                for bank, gate, opens in ((R_BANKS[h], 0, False), (N_BANKS[h], 2, True), (Z_BANKS[h], 1, False)):
                    pe.matmul(bank[:, 0:N // 2], w_ih[:, gate * H:(gate + 1) * H], agg[:, half_of(h)], start=opens,
                              stop=True, skip_group_check=True).then_inc(gates_done, 1)
            for h in range(HALVES):
                for part, ready, opens in ((x_part, x_part_ready, True), (n_part, n_part_ready, False)):
                    if opens:
                        pe.wait_ge(agg_copied, 2)
                        pe.wait_ge(tanh_r, HALVES)
                    pe.wait_ge(ready, h + 1)
                    for t in (2 * h, 2 * h + 1):
                        last = pe.matmul(y_rows(t), part[:, t * P:(t + 1) * P], ident[:, :],
                                         start=opens and Y_PLACES[t][1] == 0, stop=not opens, skip_group_check=True)
                last.then_inc(y_turned, 1)
            for u in range(2):
                stay_warm((WARM[0], WARM[1])[u])
                pe.wait_ge((x1_low, x1_high)[u], 2)
                for t in (2 * u, 2 * u + 1):
                    last = pe.transpose(X1_BANKS[u][:, (t % 2) * P:(t % 2 + 1) * P], x1[:, t, :], ident[:, :])
                last.then_inc(x1_turned, 1)

            pe.wait_ge(w_ext_ready, 1)
            pe.wait_ge(att_all_ready, 1)

            def target(u):
                half = slice(2 * u * P, 2 * (u + 1) * P)
                pe.matmul(ps_t[:, half], att2_all[:, :], x1_t[:, half], start=True, stop=True).then_inc(target_done, 1)

            def extend(u):
                for t in (2 * u, 2 * u + 1):
                    last = pe.matmul(E_BANKS[u][:, (t % 2) * (H + 1):(t % 2 + 1) * (H + 1)],
                                     x1_t[:, t * P:(t + 1) * P], w_ext[:, :], start=True, stop=True)
                last.then_inc(e_done, 1)

            pe.wait_ge(x1_t_low, 1)
            extend(0)
            target(0)
            pe.wait_ge(x1_t_high, 1)
            target(1)
            extend(1)

            def turn(t):
                pe.wait_ge(prob_ready, t + 1)
                for c in range(TILES):
                    last = pe.transpose(PROB_BANKS[t][:, c * P:(c + 1) * P], prob[:, t, c * P:(c + 1) * P],
                                        ident[:, :])
                last.then_inc(prob_turned, 1)

            def mix(t, first=0, last=TILES):
                pe.wait_ge(prob_t_ready, t + 1)
                for c in range(first, last):
                    done = pe.matmul(OUT_BANKS[t][:, 0:H], prob_t[:, t, c, :], e_ext[:, c, 0:H],
                                     start=(c == 0), stop=(c == TILES - 1), skip_group_check=True)
                if last == TILES:
                    done.then_inc(mixed, 1)

            stay_warm(WARM[2])
            turn(0)
            stay_warm(WARM[3])
            pe.wait_ge(e_low, 1)
            pe.wait_ge(e_high, 1)
            mix(0, 0, 2)
            turn(1)
            mix(0, 2, TILES)
            turn(2)
            mix(1)
            turn(3)
            mix(2)
            mix(3)


def kernel(x, adj, L0_gnn_edge_table, L0_gnn_w_ih, L0_gnn_w_hh, L0_gnn_b_ih, L0_gnn_b_hh, L1_gnn_W, L1_gnn_a):
    import numpy as np
    import concourse.bacc as bacc
    from concourse.bass_utils import run_bass_kernel_spmd

    x, adj = np.asarray(x), np.asarray(adj)
    w, a = np.asarray(L1_gnn_W), np.asarray(L1_gnn_a)
    H = x.shape[1]
    laid = {
        "x": x,
        "xT": x.T,
        "adj": adj,
        "adjT": adj.T,
        "T": np.asarray(L0_gnn_edge_table),
        "w_ihT": np.asarray(L0_gnn_w_ih).T,
        "w_hhT": np.asarray(L0_gnn_w_hh).T,
        "b_ihT": np.asarray(L0_gnn_b_ih).reshape(3, H).T,
        "b_hhT": np.asarray(L0_gnn_b_hh).reshape(3, H).T,
        "W": w,
        "WT": w.T,
        "aT": a.reshape(2, H).T,
    }
    nc = bacc.Bacc("TRN2", target_bir_lowering=False, num_devices=1)
    arrays, args = {}, {}
    for name, value in laid.items():
        value = np.ascontiguousarray(value)
        arrays[f"in_{name}"] = value
        args[name] = nc.dram_tensor(f"in_{name}", value.shape, mybir.dt.from_np(value.dtype),
                                    kind="ExternalInput").ap()
    args["out"] = nc.dram_tensor("out_x", x.shape, F32, kind="ExternalOutput").ap()
    resgnn_kernel(nc, **args)
    return run_bass_kernel_spmd(nc, [arrays], core_ids=[0]).results[0]["out_x"]
```
